# Optimizing a Trainium2 kernel written in Bass

```python
import numpy as np
import jax
import jax.numpy as jnp

def _softmax(x, axis=-1):
    return jax.nn.softmax(x, axis=axis)

def _gelu(x):
    return jax.nn.gelu(x, approximate=True)

def _silu(x):
    return jax.nn.silu(x)

def _sigmoid(x):
    return jax.nn.sigmoid(x)

def _layernorm(x, axis=-1, eps=1e-05):
    m = jnp.mean(x, axis=axis, keepdims=True)
    v = jnp.var(x, axis=axis, keepdims=True)
    return (x - m) / jnp.sqrt(v + eps)

def _scatter_add(tgt, idx, src, axis=0):
    return tgt.at[idx].add(src)

def _segment_sum(src, seg, n):
    return jax.ops.segment_sum(src, seg, n)
kernel_name = 'mk_flamingo_gated_d1_seqx_r8_49e183'

def setup_inputs(seed: int=0):
    np.random.seed(seed)
    _w = jnp.asarray

    def _rec_inputs():
        import jax
        import jax.numpy as jnp
        _rk = jax.random.key(seed)
        x = -0.0002928 + 1 * jax.random.normal(jax.random.fold_in(_rk, 1), (4, 256, 256), jnp.float32)
        _lenS = 256 - jax.random.randint(jax.random.fold_in(_rk, 7), (4,), 0, max(1, 256 // 4) + 1, jnp.int32)
        _lenS2 = 256 - jax.random.randint(jax.random.fold_in(_rk, 8), (4,), 0, max(1, 256 // 4) + 1, jnp.int32)
        _ctx_512P = jax.random.normal(jax.random.fold_in(_rk, 11), (4, 16, 64), jnp.float32)
        _ctx_512c = jax.random.dirichlet(jax.random.fold_in(_rk, 511), 0.3 * jnp.ones((16,), jnp.float32), (4, 256))
        _ctx_512t = jnp.einsum('bsk,bkd->bsd', _ctx_512c, _ctx_512P)
        _ctx_512t = _ctx_512t * jax.lax.rsqrt(jnp.mean(jnp.square(_ctx_512t)) + 1e-12) * 0.953939
        ctx_512 = 0.000227908 + 0.99994 * (_ctx_512t + 0.3 * jax.random.normal(jax.random.fold_in(_rk, 611), (4, 256, 64), jnp.float32))
        _g = jax.random.normal(jax.random.fold_in(_rk, 9001), (2, 1), jnp.float32)
        _g = jnp.sign(_g) * jnp.maximum(jnp.abs(_g), 1.0) + (_g == 0) * 1.0
        g_xattn = _g[0]
        g_ffn = _g[1]
        return (x, ctx_512, g_xattn, g_ffn)
    x, ctx_512, g_xattn, g_ffn = _rec_inputs()

    def _L0_xattn_setup():
        import jax, jax.numpy as jnp
        import numpy as np
        B, S, L = (2, 128, 128)
        DIM_Q, H, K, D_C, D_CQ, R = (256, 16, 128, 64, 192, 64)

        def _rope_tables(length, dim):
            inv = 1.0 / 10000.0 ** (jnp.arange(0, dim, 2, dtype=jnp.float32) / dim)
            f = jnp.arange(length, dtype=jnp.float32)[:, None] * inv[None, :]
            sin = jnp.repeat(jnp.sin(f), 2, axis=-1)
            cos = jnp.repeat(jnp.cos(f), 2, axis=-1)
            return (sin, cos)

        def _rotate_half(x):
            half = x.shape[-1] // 2
            return jnp.concatenate([-x[..., half:], x[..., :half]], axis=-1)

        def _apply_rope(x, sin, cos):
            return x * cos + _rotate_half(x) * sin
        key = jax.random.key(seed)
        ks = jax.random.split(key, 8)
        return {'hidden_q': jax.random.normal(ks[0], (B, S, DIM_Q), jnp.float32), 'kv_c': jax.random.normal(ks[1], (B, L, D_C), jnp.float32), 'Wq': jax.random.normal(ks[2], (H * K, DIM_Q), jnp.float32) / np.sqrt(DIM_Q).astype(np.float32), 'w_kc_q': jax.random.normal(ks[3], (H, K, D_CQ), jnp.float32) / np.sqrt(K).astype(np.float32), 'w_kc_kv': jax.random.normal(ks[4], (H, K, D_C), jnp.float32) / np.sqrt(K).astype(np.float32), 'W_qr': jax.random.normal(ks[5], (H, D_CQ, R), jnp.float32) / np.float32(np.sqrt(D_CQ) * np.sqrt(R)), 'W_kr': jax.random.normal(ks[6], (H, D_C, R), jnp.float32) / np.sqrt(D_C).astype(np.float32), 'Wo': jax.random.normal(ks[7], (DIM_Q, H * K), jnp.float32) / np.sqrt(H * K).astype(np.float32)}
    _L0_xattn_all = _L0_xattn_setup()
    _L0_xattn_in = {k: v for k, v in _L0_xattn_all.items() if k in ('Wq', 'w_kc_q', 'w_kc_kv', 'W_qr', 'W_kr', 'Wo')}
    del _L0_xattn_all

    def _L0_ffn_setup():
        import jax, jax.numpy as jnp
        import numpy as np
        TOP_K = 8
        key = jax.random.key(seed)
        k1, k2, k3 = jax.random.split(key, 3)
        B, S, H, E = (4, 512, 256, 64)
        hidden_states = jax.random.normal(k1, (B, S, H), dtype=jnp.float32)
        router_weight = jax.random.normal(k2, (E, H), dtype=jnp.float32)
        router_bias = jnp.zeros((E,), dtype=jnp.float32)
        expert_bias = jax.random.normal(k3, (E, H), dtype=jnp.float32) * 0.1
        return {'hidden_states': hidden_states, 'router_weight': router_weight, 'router_bias': router_bias, 'expert_bias': expert_bias}
    _L0_ffn_all = _L0_ffn_setup()
    _L0_ffn_in = {k: v for k, v in _L0_ffn_all.items() if k in ('router_weight', 'router_bias', 'expert_bias')}
    del _L0_ffn_all
    return {'x': x, 'ctx_512': ctx_512, 'g_xattn': g_xattn, 'g_ffn': g_ffn, 'L0_xattn_Wq': _L0_xattn_in['Wq'], 'L0_xattn_w_kc_q': _L0_xattn_in['w_kc_q'], 'L0_xattn_w_kc_kv': _L0_xattn_in['w_kc_kv'], 'L0_xattn_W_qr': _L0_xattn_in['W_qr'], 'L0_xattn_W_kr': _L0_xattn_in['W_kr'], 'L0_xattn_Wo': _L0_xattn_in['Wo'], 'L0_ffn_router_weight': _L0_ffn_in['router_weight'], 'L0_ffn_router_bias': _L0_ffn_in['router_bias'], 'L0_ffn_expert_bias': _L0_ffn_in['expert_bias']}

def reference(x, ctx_512, g_xattn, g_ffn, L0_xattn_Wq, L0_xattn_w_kc_q, L0_xattn_w_kc_kv, L0_xattn_W_qr, L0_xattn_W_kr, L0_xattn_Wo, L0_ffn_router_weight, L0_ffn_router_bias, L0_ffn_expert_bias):
    import jax
    import jax.numpy as jnp

    def _L0_xattn_ref(hidden_q, kv_c, Wq, w_kc_q, w_kc_kv, W_qr, W_kr, Wo):
        import jax, jax.numpy as jnp
        import numpy as np
        B, S, L = (2, 128, 128)
        DIM_Q, H, K, D_C, D_CQ, R = (256, 16, 128, 64, 192, 64)

        def _rope_tables(length, dim):
            inv = 1.0 / 10000.0 ** (jnp.arange(0, dim, 2, dtype=jnp.float32) / dim)
            f = jnp.arange(length, dtype=jnp.float32)[:, None] * inv[None, :]
            sin = jnp.repeat(jnp.sin(f), 2, axis=-1)
            cos = jnp.repeat(jnp.cos(f), 2, axis=-1)
            return (sin, cos)

        def _rotate_half(x):
            half = x.shape[-1] // 2
            return jnp.concatenate([-x[..., half:], x[..., :half]], axis=-1)

        def _apply_rope(x, sin, cos):
            return x * cos + _rotate_half(x) * sin
        Bv, Sv, _ = hidden_q.shape
        _, Lv, _ = kv_c.shape
        q_hk = (hidden_q @ Wq.T).reshape(Bv, Sv, H, K)
        q_big = jnp.einsum('bshk,hkq->bshq', q_hk, w_kc_q)
        sin_q, cos_q = _rope_tables(Sv, D_CQ)
        q_big = _apply_rope(q_big, sin_q[None, :, None, :], cos_q[None, :, None, :])
        sin_k, cos_k = _rope_tables(Lv, D_C)
        kv_r = _apply_rope(kv_c, sin_k[None], cos_k[None])
        q_r = jnp.einsum('bshq,hqr->bhsr', q_big, W_qr)
        k_r = jnp.einsum('bld,hdr->bhlr', kv_r, W_kr)
        scores = jnp.einsum('bhsr,bhlr->bhsl', q_r, k_r)
        attn = jax.nn.softmax(scores, axis=-1)
        ctx_c = jnp.einsum('bhsl,bld->bhsd', attn, kv_r)
        ctx_lat = jnp.einsum('bhsd,hkd->bhsk', ctx_c, w_kc_kv)
        ctx = ctx_lat.transpose(0, 2, 1, 3).reshape(Bv, Sv, H * K)
        return ctx @ Wo.T

    def _L0_ffn_ref(hidden_states, router_weight, router_bias, expert_bias):
        import jax, jax.numpy as jnp
        import numpy as np
        TOP_K = 8
        B, S, H = hidden_states.shape
        flat = hidden_states.reshape(B * S, H)
        logits = jnp.einsum('th,eh->te', flat, router_weight) + router_bias
        scores = jax.nn.softmax(logits, axis=-1)
        topk_w, topk_idx = jax.lax.top_k(scores, TOP_K)
        gathered_bias = expert_bias[topk_idx]
        out = flat * jnp.sum(topk_w, axis=-1, keepdims=True) + jnp.einsum('tk,tkh->th', topk_w, gathered_bias)
        return out.reshape(B, S, H)
    x = x + jnp.tanh(g_xattn[0]) * _L0_xattn_ref(_layernorm(x, axis=-1), ctx_512, L0_xattn_Wq, L0_xattn_w_kc_q, L0_xattn_w_kc_kv, L0_xattn_W_qr, L0_xattn_W_kr, L0_xattn_Wo)
    x = x + jnp.tanh(g_ffn[0]) * _L0_ffn_ref(_layernorm(x, axis=-1), L0_ffn_router_weight, L0_ffn_router_bias, L0_ffn_expert_bias)
    return x

_drawn_inputs = setup_inputs


def setup_inputs(seed=0):
    import zlib

    import numpy as np

    out = dict(_drawn_inputs(seed))
    spreads = {'L0_ffn_router_bias': (0.0, 0.513)}
    factors = {}
    for name, (base, spread) in spreads.items():
        noise = np.random.default_rng([zlib.crc32(name.encode()), seed]).standard_normal(out[name].shape)
        drawn = base * np.exp(spread * noise) if base else spread * noise
        out[name] = jnp.asarray(drawn.astype(out[name].dtype))
    for name, factor in factors.items():
        out[name] = (out[name] * factor).astype(out[name].dtype)
    return out
```

```python
from contextlib import ExitStack

import numpy as np

import concourse.bass as bass
from concourse import mybir

P = 128
F32 = mybir.dt.float32
F32R = mybir.dt.float32r
ALU = mybir.AluOpType
ACT = mybir.ActivationFunctionType
AX_X = mybir.AxisListType.X

B, S, D = 4, 256, 256
L, DC = 256, 64
H, K, CQ, R = 16, 128, 192, 64
E, TOP = 64, 8
EPS = 1e-5
TOKENS = B * S
CHUNKS = TOKENS // P

HALF = CQ // 2
GH = 4
GROUPS = H // GH
PC = GH * HALF // P
SPAN = 512
STEPS = GROUPS * TOKENS // SPAN
ITEMS = GH * 2
PAIRS = H // 2
RING = 4
E_BUFS, T_BUFS = 4, 4
LEAD = 2


def ring_plan():
    def weights(g):
        return [("a", g, hh) for hh in range(GH)] + [("m", g, 0), ("m", g, 1), ("o", g, 0)]

    def queries(n):
        return [("q", n, k, j) for k in range(PC) for j in range(2)]

    before = [("x", t, dc) for t in range(2) for dc in range(2)] + [("k", i) for i in range(2)]
    before += weights(0) + queries(0) + [("r", 0), ("p", 0)]
    steps = []
    for n in range(STEPS):
        slots = [[] for _ in range(ITEMS)]
        if n + 1 < STEPS:
            q = queries(n + 1)
            slots[0], slots[1], slots[2], slots[3] = q[0:2], q[2:4], q[4:5], q[5:6]
            slots[4], slots[5] = [("r", n + 1)], [("p", n + 1)]
        if n % 2 == 0 and n // 2 + 1 < GROUPS:
            w = weights(n // 2 + 1)
            slots[2] = slots[2] + w[0:1]
            slots[3] = slots[3] + w[1:2]
            slots[4] = w[2:3] + slots[4]
            slots[6], slots[7] = w[3:5], w[5:7]
        steps.append(slots)
    return before, steps


def number(before, steps):
    used = 0

    def take(pieces):
        nonlocal used
        out = []
        for piece in pieces:
            out.append((used, piece))
            used += 1
        return out

    before = take(before)
    steps = [[take(slot) for slot in slots] for slots in steps]
    return before, steps, used


def flamingo_gated_layer(nc, x, ctx, gate_attn, gate_ffn, wq, w_kc_q, w_kc_kv, w_qr, w_kr, wo_t,
                         router_t, router_b, expert_b, rope_q, rope_k, out):
    before, steps, ring_used = number(*ring_plan())
    items = STEPS * ITEMS

    order = [q for _, q in before] + [q for slots in steps for slot in slots for _, q in slot]
    hi_count, count = {}, 0
    for piece in order:
        if piece[0] in "xkap":
            hi_count[piece] = count + 1
            count += 2 if piece[0] == "p" else 1

    with ExitStack() as stack:
        def sb(name, shape, dt=F32):
            return stack.enter_context(nc.sbuf_tensor(name, shape, dt))

        def psum(name, shape):
            return stack.enter_context(nc.psum_tensor(name, shape, F32))

        def sem(name):
            return stack.enter_context(nc.semaphore(name))

        ring = psum("ring", [P, RING, 512])
        scores = psum("scores", [P, 2, 2, L])
        probs_t = psum("probs_t", [P, 2, S])
        context = psum("context", [P, 512])

        x_sb = sb("x_sb", [P, CHUNKS, D])
        ctx_sb = sb("ctx_sb", [P, CHUNKS, DC])
        gates = sb("gates", [P, 2])
        rope_q_sb = sb("rope_q_sb", [P, PC, 4, S])
        rope_k_sb = sb("rope_k_sb", [P, 2, 2, DC])
        wq_sb = sb("wq_sb", [P, GH, D])
        w_kc_q_sb = sb("w_kc_q_sb", [P, GH, CQ])
        w_kc_kv_sb = sb("w_kc_kv_sb", [P, GH, DC])
        wo_t_sb = sb("wo_t_sb", [P, GH, D])
        w_qr_sb = sb("w_qr_sb", [P, 2, PC, P])
        w_kr_sb = sb("w_kr_sb", [P, PC, P])
        router_t_sb = sb("router_t_sb", [P, 2, E])
        router_b_sb = sb("router_b_sb", [1, E])
        expert_b_sb = sb("expert_b_sb", [E, D])

        ident = sb("ident", [P, P])
        ones = sb("ones", [1, P])
        minus_half = sb("minus_half", [P, CHUNKS])
        tanh_gates = sb("tanh_gates", [P, 2])
        stats = sb("stats", [P, CHUNKS, 6])
        moments = sb("moments", [P, CHUNKS, 2])
        var_eps = sb("var_eps", [P, CHUNKS])
        rstd = sb("rstd", [P, CHUNKS])
        neg_max = sb("neg_max", [P, 4, 2])
        row_sum = sb("row_sum", [P, 4, 2])
        inv_sum = sb("inv_sum", [P, 4, 2])

        xn_hi = sb("xn_hi", [P, 2, TOKENS], F32R)
        xn_lo = sb("xn_lo", [P, 2, TOKENS], F32R)
        a_hi = sb("a_hi", [P, 2, 2, 2, GH * HALF], F32R)
        a_lo = sb("a_lo", [P, 2, 2, 2, GH * HALF], F32R)
        keys_hi = sb("keys_hi", [P, B * L], F32R)
        keys_lo = sb("keys_lo", [P, B * L], F32R)
        q_stack = sb("q_stack", [P, GH, SPAN], F32R)

        keys = sb("keys", [P, CHUNKS, 2, DC])
        m_sb = sb("m_sb", [P, 2, 2, PC, P])
        o_sb = sb("o_sb", [P, PAIRS, D])
        roped = sb("roped", [P, 2, PC, SPAN])
        cross = sb("cross", [P, 2, 2, SPAN])
        probs = sb("probs", [P, E_BUFS, 2, L])
        probs_t_sb = sb("probs_t_sb", [P, T_BUFS, 2, S])
        context_t = sb("context_t", [P, PAIRS, TOKENS])
        xn = context_t[:, 0:2, :].rearrange("p a (c d) -> p (a c) d", d=D)

        xn2 = roped[:, :, :, :].rearrange("p a b c -> p (a b c)")[:, 0:TOKENS * D // P].rearrange(
            "p (c d) -> p c d", d=D)
        xn2_t = sb("xn2_t", [P, 2, 2, P])
        expo = sb("expo", [P, 2, E])
        rest = sb("rest", [P, 2, E])
        taken = sb("taken", [P, 2, E])
        taken_t = sb("taken_t", [E, 2, P])
        neg_max2 = sb("neg_max2", [P, CHUNKS])
        sum2 = sb("sum2", [P, CHUNKS])
        inv2 = sb("inv2", [P, CHUNKS])
        top8 = sb("top8", [P, CHUNKS, TOP])
        top_sum = sb("top_sum", [P, CHUNKS])
        scale_e = sb("scale_e", [P, CHUNKS])
        scale_x = sb("scale_x", [P, CHUNKS])
        y = sb("y", [P, 2, D])

        x_in = [sem(f"x_in{i}") for i in range(4)]
        ctx_in = sem("ctx_in")
        rope_k_in = sem("rope_k_in")
        rope_q_in = sem("rope_q_in")
        gates_in = sem("gates_in")
        ffn_in = sem("ffn_in")
        weights_in = [sem(f"weights_in{g}") for g in range(GROUPS)]
        stored = sem("stored")
        filled = sem("filled")
        gated = sem("gated")
        stats_ready = sem("stats_ready")
        moments_ready = sem("moments_ready")
        var_ready = sem("var_ready")
        rstd_ready = sem("rstd_ready")
        xn_ready = sem("xn_ready")
        key_products = sem("key_products")
        keys_ready = sem("keys_ready")
        ring_full = sem("ring_full")
        ring_free = sem("ring_free")
        hi_ready = sem("hi_ready")
        lo_ready = sem("lo_ready")
        merged = sem("merged")
        rope_ready = sem("rope_ready")
        scores_ready = sem("scores_ready")
        max_ready = sem("max_ready")
        exp_ready = sem("exp_ready")
        inv_ready = sem("inv_ready")
        probs_ready = sem("probs_ready")
        transposed = sem("transposed")
        probs_t_ready = sem("probs_t_ready")
        context_ready = sem("context_ready")
        context_copied = sem("context_copied")
        x1_ready = sem("x1_ready")
        stats2_ready = sem("stats2_ready")
        moments2_ready = sem("moments2_ready")
        var2_ready = sem("var2_ready")
        rstd2_ready = sem("rstd2_ready")
        xn2_ready = sem("xn2_ready")
        xn2_turned = sem("xn2_turned")
        xn2_t_ready = sem("xn2_t_ready")
        logits_ready = sem("logits_ready")
        max2_ready = sem("max2_ready")
        exp2_ready = sem("exp2_ready")
        top8_ready = sem("top8_ready")
        rest_ready = sem("rest_ready")
        taken_ready = sem("taken_ready")
        taken_turned = sem("taken_turned")
        taken_t_ready = sem("taken_t_ready")
        scales = sem("scales")
        partial = sem("partial")
        y_ready = sem("y_ready")

        def bank(u):
            return ring[:, u % RING, :]

        def item_of(i):
            n, s = divmod(i, ITEMS)
            return n, 2 * (s // 4) + s % 2, (s // 2) % 2

        n_ring = ring_used

        def out_use(c):
            return n_ring + c + max(0, min(c - 4, CHUNKS) + 1 if c >= 4 else 0)

        def acc_use(c):
            slot = c + 4
            return n_ring + min(slot, CHUNKS) + c

        weights_end = [
            1 + max(u for u, p in before + [q for slots in steps for slot in slots for q in slot]
                    if p[0] in "amo" and p[1] == g)
            for g in range(GROUPS)
        ]

        block = stack.enter_context(nc.Block())

        @block.sync
        def _(sp):
            x_dram = x.rearrange("(c p) d -> p c d", p=P)
            for i in range(4):
                sp.dma_start(x_sb[:, 2 * i:2 * i + 2, :], x_dram[:, 2 * i:2 * i + 2, :]).then_inc(x_in[i], 16)
            for g in range(GROUPS):
                if g:
                    sp.wait_ge(ring_full, weights_end[g - 1])
                heads = slice(g * GH, (g + 1) * GH)
                for dst, src in (
                    (wq_sb[:], wq[heads].rearrange("h k d -> k h d")),
                    (w_kc_q_sb[:], w_kc_q[heads].rearrange("h k c -> k h c")),
                    (w_qr_sb[:], w_qr[g]),
                    (w_kr_sb[:], w_kr[g]),
                    (w_kc_kv_sb[:], w_kc_kv[heads].rearrange("h k d -> k h d")),
                    (wo_t_sb[:], wo_t[heads].rearrange("h k d -> k h d")),
                ):
                    sp.dma_start(dst, src).then_inc(weights_in[g], 16)
            for c in range(CHUNKS):
                sp.wait_ge(y_ready, c + 1)
                sp.dma_start(out[c * P:(c + 1) * P, :], y[:, c % 2, :]).then_inc(stored, 16)
            sp.wait_ge(stored, 16 * CHUNKS)

        @block.gpsimd
        def _(pool):
            nc.gpsimd.memset(ident[:], 0.0).then_inc(filled, 1)
            nc.gpsimd.memset(ones[:], 1.0).then_inc(filled, 1)
            nc.gpsimd.memset(minus_half[:], -0.5).then_inc(filled, 1)
            pool.wait_ge(filled, 3)
            nc.gpsimd.affine_select(out=ident[:], in_=ident[:], compare_op=ALU.not_equal, fill=1.0, base=0,
                                    pattern=[[-1, P]], channel_multiplier=1).then_inc(filled, 1)
            for i in range(4):
                pool.wait_ge(var_ready, i + 1)
                nc.gpsimd.tensor_tensor(rstd[:, 2 * i:2 * i + 2], var_eps[:, 2 * i:2 * i + 2],
                                        minus_half[:, 0:2], ALU.pow).then_inc(rstd_ready, 1)

            def rope_sums(n, k, u):
                done = n * PC + k
                pool.wait_ge(ring_free, u + 1)
                for j in range(2):
                    last = nc.gpsimd.tensor_tensor(roped[:, j, k, :], roped[:, j, k, :],
                                                   cross[:, done % 2, j, :], ALU.add)
                last.then_inc(rope_ready, 1)

            def pieces(slot):
                for u, piece in slot:
                    if piece[0] == "q" and piece[3] == 1:
                        rope_sums(piece[1], piece[2], u)

            def normalise(i):
                pool.wait_ge(inv_ready, i + 1)
                for half in range(2):
                    e = probs[:, i % E_BUFS, half, :]
                    last = nc.gpsimd.tensor_scalar(e, e, inv_sum[:, i % 4, half:half + 1], 1.0,
                                                   ALU.mult, ALU.mult)
                last.then_inc(probs_ready, 1)

            pieces(before)
            normalise(0)
            for n in range(STEPS):
                for s in range(ITEMS):
                    if n * ITEMS + s + 1 < items:
                        normalise(n * ITEMS + s + 1)
                    pieces(steps[n][s])
            for c in range(CHUNKS):
                pool.wait_ge(var2_ready, c + 1)
                nc.gpsimd.tensor_tensor(rstd[:, c:c + 1], var_eps[:, c:c + 1], minus_half[:, 0:1],
                                        ALU.pow).then_inc(rstd2_ready, 1)

        @block.scalar
        def _(act):
            ctx_dram = ctx.rearrange("(c p) d -> p c d", p=P)
            act.dma_start(ctx_sb[:], ctx_dram).then_inc(ctx_in, 16)
            act.dma_start(rope_k_sb[:], rope_k).then_inc(rope_k_in, 16)
            act.dma_start(gates[:, 0:1], gate_attn.rearrange("(o a) -> o a", o=1).broadcast_to([P, 1])).then_inc(gates_in, 16)
            act.dma_start(gates[:, 1:2], gate_ffn.rearrange("(o a) -> o a", o=1).broadcast_to([P, 1])).then_inc(gates_in, 16)
            act.dma_start(rope_q_sb[:], rope_q).then_inc(rope_q_in, 16)
            act.dma_start(router_t_sb[:], router_t.rearrange("(c p) e -> p c e", p=P)).then_inc(ffn_in, 16)
            act.dma_start(router_b_sb[:], router_b.rearrange("(o e) -> o e", o=1)).then_inc(ffn_in, 16)
            act.dma_start(expert_b_sb[:], expert_b).then_inc(ffn_in, 16)
            act.wait_ge(gates_in, 32)
            nc.scalar.activation(tanh_gates[:], gates[:], ACT.Tanh).then_inc(gated, 1)

            def pieces(slot):
                for u, piece in slot:
                    kind = piece[0]
                    if kind not in "xkap":
                        continue
                    if kind == "p":
                        stack_queries(u, piece[1])
                        continue
                    act.wait_ge(ring_full, u + 1)
                    if kind == "x":
                        _, t, dc = piece
                        nc.scalar.copy(xn_hi[:, dc, t * SPAN:(t + 1) * SPAN], bank(u)).then_inc(hi_ready, 1)
                    elif kind == "k":
                        i = piece[1]
                        nc.scalar.copy(keys_hi[:, i * 512:(i + 1) * 512], bank(u)).then_inc(hi_ready, 1)
                    else:
                        _, g, hh = piece
                        src = bank(u)[:, 0:2 * CQ].rearrange("p (c j r) -> p c j r", c=2, j=2)
                        dst = a_hi[:, g % 2, :, :, hh * HALF:(hh + 1) * HALF]
                        nc.scalar.copy(dst, src).then_inc(hi_ready, 1)

            def stack_queries(u, n):
                for pair in range(2):
                    act.wait_ge(ring_full, u + pair)
                    if n:
                        act.wait_ge(scores_ready, (n - 1) * ITEMS + 4 * pair + 4)
                    nc.scalar.copy(q_stack[0:64, 2 * pair, :], bank(u - 1 + pair)[0:64, :])
                    last = nc.scalar.copy(q_stack[64:128, 2 * pair + 1, :], bank(u - 1 + pair)[64:128, :])
                    last.then_inc(hi_ready, 1)

            def exponentials(i):
                act.wait_ge(max_ready, i + 1)
                if i >= E_BUFS:
                    act.wait_ge(transposed, i - E_BUFS + 1)
                for half in range(2):
                    last = nc.scalar.activation(probs[:, i % E_BUFS, half, :], scores[:, i % 2, half, :], ACT.Exp,
                                                bias=neg_max[:, i % 4, half:half + 1],
                                                accum_out=row_sum[:, i % 4, half:half + 1])
                last.then_inc(exp_ready, 1)

            def copy_transposed(i):
                act.wait_ge(transposed, i + 1)
                if i >= T_BUFS:
                    act.wait_ge(context_ready, (i - T_BUFS) // 2 + 1)
                nc.scalar.copy(probs_t_sb[:, i % T_BUFS], probs_t[:]).then_inc(probs_t_ready, 1)

            def copy_context(q):
                n, head, b = item_of(2 * q)
                act.wait_ge(context_ready, q + 1)
                tok = (n % 2) * SPAN + b * S
                nc.scalar.copy(context_t[:, (n // 2) * 2 + head // 2, tok:tok + S],
                               context[:, 0:S]).then_inc(context_copied, 1)

            pieces(before)
            for i in range(LEAD):
                exponentials(i)
            for n in range(STEPS):
                for s in range(ITEMS):
                    i = n * ITEMS + s
                    if i >= 3 and i % 2 == 1:
                        copy_context(i // 2 - 1)
                    pieces(steps[n][s])
                    copy_transposed(i)
                    if i + LEAD < items:
                        exponentials(i + LEAD)
            copy_context(items // 2 - 1)

            for slot in range(CHUNKS + 4):
                c = slot - 3
                if 0 <= c < CHUNKS:
                    act.wait_ge(taken_turned, c + 1)
                    nc.scalar.copy(taken_t[:, c % 2, :], context[0:E, 0:P]).then_inc(taken_t_ready, 1)
                c = slot - 2
                if 0 <= c < CHUNKS:
                    act.wait_ge(max2_ready, c + 1)
                    if c >= 2:
                        act.wait_ge(taken_ready, c - 1)
                    nc.scalar.activation(expo[:, c % 2, :], probs_t[:, 0, 0:E], ACT.Exp,
                                         bias=neg_max2[:, c:c + 1],
                                         accum_out=sum2[:, c:c + 1]).then_inc(exp2_ready, 1)
                c = slot - 1
                if 0 <= c < CHUNKS:
                    act.wait_ge(xn2_turned, c + 1)
                    nc.scalar.copy(xn2_t[:, c % 2], scores[:, c % 2, 0, :].rearrange("p (a b) -> p a b", a=2)
                                   ).then_inc(xn2_t_ready, 1)

        @block.vector
        def _(dve):
            for i in range(4):
                dve.wait_ge(x_in[i], 16)
                for c in (2 * i, 2 * i + 1):
                    last = nc.vector.bn_stats(stats[:, c, :], x_sb[:, c, :])
                last.then_inc(stats_ready, 1)
                dve.wait_ge(stats_ready, i + 1)
                for c in (2 * i, 2 * i + 1):
                    last = nc.vector.bn_aggr(moments[:, c, :], stats[:, c, :])
                last.then_inc(moments_ready, 1)
                dve.wait_ge(moments_ready, i + 1)
                nc.vector.tensor_scalar(var_eps[:, 2 * i:2 * i + 2], moments[:, 2 * i:2 * i + 2, 1], EPS, None,
                                        ALU.add).then_inc(var_ready, 1)
            for i in range(4):
                dve.wait_ge(rstd_ready, i + 1)
                for c in (2 * i, 2 * i + 1):
                    last = nc.vector.tensor_scalar(xn[:, c, :], x_sb[:, c, :], moments[:, c, 0:1], rstd[:, c:c + 1],
                                                   ALU.subtract, ALU.mult)
                last.then_inc(xn_ready, 1)

            dve.wait_ge(ctx_in, 16)
            dve.wait_ge(rope_k_in, 16)
            hk = DC // 2
            for b in range(B):
                c = slice(2 * b, 2 * b + 2)
                nc.vector.tensor_tensor(keys[:, c, 0, :], ctx_sb[:, c, :], rope_k_sb[:, :, 0, :], ALU.mult)
                nc.vector.tensor_tensor(keys[:, c, 1, 0:hk], ctx_sb[:, c, hk:DC], rope_k_sb[:, :, 1, 0:hk], ALU.mult)
                last = nc.vector.tensor_tensor(keys[:, c, 1, hk:DC], ctx_sb[:, c, 0:hk], rope_k_sb[:, :, 1, hk:DC],
                                               ALU.mult)
            last.then_inc(key_products, 1)
            dve.wait_ge(key_products, 1)
            nc.vector.tensor_tensor(keys[:, :, 0, :], keys[:, :, 0, :], keys[:, :, 1, :], ALU.add
                                    ).then_inc(key_products, 1)
            dve.wait_ge(key_products, 2)
            nc.vector.tensor_copy(keys[:, :, 1, :], keys[:, :, 0, :]).then_inc(keys_ready, 1)

            def low(dst, src, hi, piece, extra=0):
                dve.wait_ge(hi_ready, hi_count[piece] + extra)
                return nc.vector.tensor_tensor(dst, src, hi.bitcast(F32), ALU.subtract)

            def rope(n, k, j, u):
                done = n * PC + k
                if j == 0 and done >= 2:
                    dve.wait_ge(rope_ready, done - 1)
                if done == 0 and j == 0:
                    dve.wait_ge(rope_q_in, 16)
                dve.wait_ge(ring_full, u + 1)
                q = bank(u).rearrange("p (b s) -> p b s", b=2)
                straight = rope_q_sb[:, k, 2 * j:2 * j + 1, :].broadcast_to([P, 2, S])
                crossed = rope_q_sb[:, k, 3 - 2 * j:4 - 2 * j, :].broadcast_to([P, 2, S])
                nc.vector.tensor_tensor(roped[:, j, k, :].rearrange("p (b s) -> p b s", b=2), q, straight, ALU.mult)
                last = nc.vector.tensor_tensor(cross[:, done % 2, 1 - j, :].rearrange("p (b s) -> p b s", b=2), q,
                                               crossed, ALU.mult)
                last.then_inc(ring_free, 1)

            def pieces(slot):
                for u, piece in slot:
                    kind = piece[0]
                    if kind == "x":
                        _, t, dc = piece
                        cols = slice(t * SPAN, (t + 1) * SPAN)
                        last = low(xn_lo[:, dc, cols], bank(u), xn_hi[:, dc, cols], piece)
                        last.then_inc(ring_free, 1)
                    elif kind == "k":
                        cols = slice(piece[1] * 512, (piece[1] + 1) * 512)
                        low(keys_lo[:, cols], bank(u), keys_hi[:, cols], piece).then_inc(ring_free, 1)
                    elif kind == "a":
                        _, g, hh = piece
                        at = (slice(None), g % 2, slice(None), slice(None), slice(hh * HALF, (hh + 1) * HALF))
                        src = bank(u)[:, 0:2 * CQ].rearrange("p (c j r) -> p c j r", c=2, j=2)
                        low(a_lo[at], src, a_hi[at], piece).then_inc(ring_free, 1)
                    elif kind == "m":
                        _, g, j = piece
                        dve.wait_ge(ring_full, u + 1)
                        nc.vector.tensor_copy(m_sb[:, g % 2, j, :, :],
                                              bank(u)[:, 0:PC * P].rearrange("p (k c) -> p k c", k=PC)
                                              ).then_inc(ring_free, 1)
                    elif kind == "o":
                        g = piece[1]
                        if g == 0:
                            dve.wait_ge(gated, 1)
                        dve.wait_ge(ring_full, u + 1)
                        nc.vector.tensor_scalar(o_sb[:, 2 * g:2 * g + 2, :],
                                                bank(u).rearrange("p (a d) -> p a d", a=2),
                                                tanh_gates[:, 0:1], None, ALU.mult).then_inc(ring_free, 1)
                    elif kind == "q":
                        _, n, k, j = piece
                        rope(n, k, j, u)
                    elif kind == "p":
                        for pair in range(2):
                            h0, h1 = 2 * pair, 2 * pair + 1
                            b = bank(u - 1 + pair)
                            low(q_stack[64:128, h0, :], b[0:64, :], q_stack[0:64, h0, :], piece, pair)
                            low(q_stack[0:64, h1, :], b[64:128, :], q_stack[64:128, h1, :], piece, pair
                                ).then_inc(ring_free, 1)

            def maxima(i):
                dve.wait_ge(scores_ready, i + 1)
                nc.vector.tensor_reduce(neg_max[:, i % 4, :], scores[:, i % 2], AX_X, ALU.max,
                                        negate=True).then_inc(max_ready, 1)

            def inverse(i):
                dve.wait_ge(exp_ready, i + 1)
                nc.vector.reciprocal(inv_sum[:, i % 4, :], row_sum[:, i % 4, :]).then_inc(inv_ready, 1)

            pieces(before)
            for i in range(LEAD):
                maxima(i)
            inverse(0)
            for n in range(STEPS):
                for s in range(ITEMS):
                    i = n * ITEMS + s
                    if i + 1 < items:
                        inverse(i + 1)
                    if i + LEAD < items and s != 6:
                        maxima(i + LEAD)
                    pieces(steps[n][s])
                    if i + LEAD < items and s == 6:
                        maxima(i + LEAD)

            for slot in range(CHUNKS + 5):
                c = slot - 4
                if 0 <= c < CHUNKS:
                    dve.wait_ge(ring_full, acc_use(c) + 1)
                    dve.wait_ge(partial, c + 1)
                    nc.vector.scalar_tensor_tensor(out=y[:, c % 2, :], in0=bank(acc_use(c))[:, 0:D],
                                                   scalar=scale_e[:, c:c + 1], in1=y[:, c % 2, :],
                                                   op0=ALU.mult, op1=ALU.add).then_inc(y_ready, 1)
                c = slot
                if c < CHUNKS:
                    dve.wait_ge(ring_full, out_use(c) + 1)
                    nc.vector.tensor_tensor(x_sb[:, c, :], bank(out_use(c))[:, 0:D], x_sb[:, c, :], ALU.add
                                            ).then_inc(x1_ready, 1)
                    dve.wait_ge(x1_ready, c + 1)
                    nc.vector.bn_stats(stats[:, c, :], x_sb[:, c, :]).then_inc(stats2_ready, 1)
                    dve.wait_ge(stats2_ready, c + 1)
                    nc.vector.bn_aggr(moments[:, c, :], stats[:, c, :]).then_inc(moments2_ready, 1)
                    dve.wait_ge(moments2_ready, c + 1)
                    nc.vector.tensor_scalar(var_eps[:, c:c + 1], moments[:, c, 1:2], EPS, None, ALU.add
                                            ).then_inc(var2_ready, 1)
                c = slot - 2
                if 0 <= c < CHUNKS:
                    dve.wait_ge(logits_ready, c + 1)
                    nc.vector.tensor_reduce(neg_max2[:, c:c + 1], probs_t[:, 0, 0:E], AX_X, ALU.max,
                                            negate=True).then_inc(max2_ready, 1)
                c = slot
                if c < CHUNKS:
                    dve.wait_ge(rstd2_ready, c + 1)
                    nc.vector.tensor_scalar(xn2[:, c, :], x_sb[:, c, :], moments[:, c, 0:1], rstd[:, c:c + 1],
                                            ALU.subtract, ALU.mult).then_inc(xn2_ready, 1)
                c = slot - 2
                if 0 <= c < CHUNKS:
                    dve.wait_ge(exp2_ready, c + 1)
                    nc.vector.max(top8[:, c, :], expo[:, c % 2, :]).then_inc(top8_ready, 1)
                    dve.wait_ge(top8_ready, c + 1)
                    nc.vector.match_replace(out=rest[:, c % 2, :], in_to_replace=top8[:, c, :],
                                            in_values=expo[:, c % 2, :], imm_value=0.0).then_inc(rest_ready, 1)
                    nc.vector.tensor_reduce(top_sum[:, c:c + 1], top8[:, c, :], AX_X, ALU.add).then_inc(scales, 1)
                    nc.vector.reciprocal(inv2[:, c:c + 1], sum2[:, c:c + 1]).then_inc(scales, 1)
                    dve.wait_ge(rest_ready, c + 1)
                    if c >= 2:
                        dve.wait_ge(taken_turned, c - 1)
                    nc.vector.tensor_tensor(taken[:, c % 2, :], expo[:, c % 2, :], rest[:, c % 2, :], ALU.subtract
                                            ).then_inc(taken_ready, 1)
                    dve.wait_ge(scales, 4 * c + 2)
                    nc.vector.tensor_tensor(scale_e[:, c:c + 1], inv2[:, c:c + 1], tanh_gates[:, 1:2], ALU.mult
                                            ).then_inc(scales, 1)
                    dve.wait_ge(scales, 4 * c + 3)
                    nc.vector.tensor_tensor(scale_x[:, c:c + 1], scale_e[:, c:c + 1], top_sum[:, c:c + 1], ALU.mult
                                            ).then_inc(scales, 1)
                    dve.wait_ge(scales, 4 * c + 4)
                    if c >= 2:
                        dve.wait_ge(stored, 16 * (c - 1))
                    nc.vector.scalar_tensor_tensor(out=y[:, c % 2, :], in0=xn2[:, c, :], scalar=scale_x[:, c:c + 1],
                                                   in1=x_sb[:, c, :], op0=ALU.mult, op1=ALU.add
                                                   ).then_inc(partial, 1)

        ready = {}
        for u, piece in before + [q for slots in steps for slot in slots for q in slot]:
            ready[piece] = u + 1

        @block.tensor
        def _(pe):
            def free(u):
                if u >= RING:
                    pe.wait_ge(ring_free, u - RING + 1)

            def piece_done(u, last):
                last.then_inc(ring_full, 1)

            def turn_x(u, t, dc):
                for i in range(4):
                    c = 4 * t + i
                    pe.wait_ge(xn_ready, c // 2 + 1)
                    last = nc.tensor.transpose(bank(u)[:, i * P:(i + 1) * P], xn[:, c, dc * P:(dc + 1) * P], ident[:])
                piece_done(u, last)

            def turn_keys(u, i):
                pe.wait_ge(keys_ready, 1)
                for c in range(4):
                    last = nc.tensor.transpose(bank(u)[:, c * P:(c + 1) * P],
                                               keys[:, 4 * i + c].rearrange("p a d -> p (a d)"), ident[:])
                piece_done(u, last)

            def merge_queries(u, g, hh):
                pe.wait_ge(weights_in[g], 96)
                for dc in range(2):
                    last = nc.tensor.matmul(bank(u)[:, dc * CQ:(dc + 1) * CQ], wq_sb[:, hh, dc * P:(dc + 1) * P],
                                            w_kc_q_sb[:, hh, :], start=True, stop=True)
                piece_done(u, last)

            def merge_ranks(u, g, j):
                for k in range(PC):
                    last = nc.tensor.matmul(bank(u)[:, k * P:(k + 1) * P], w_qr_sb[:, j, k, :], w_kr_sb[:, k, :],
                                            start=True, stop=True)
                piece_done(u, last)

            def merge_outputs(u, g):
                for pair in range(2):
                    for e in range(2):
                        hh = 2 * pair + e
                        last = nc.tensor.matmul(bank(u)[64 * e:64 * e + 64, pair * D:(pair + 1) * D],
                                                w_kc_kv_sb[:, hh, :], wo_t_sb[:, hh, :], start=True, stop=True)
                piece_done(u, last)

            def project(u, n, k, j):
                g, t = n // 2, n % 2
                pe.wait_ge(ring_free, ready[("a", g, GH - 1)])
                pe.wait_ge(ring_free, ready[("x", t, 1)])
                cols = slice(t * SPAN, (t + 1) * SPAN)
                terms = [(a, xx, dc) for dc in range(2) for a, xx in ((a_hi, xn_hi), (a_hi, xn_lo), (a_lo, xn_hi))]
                for i, (a, xx, dc) in enumerate(terms):
                    last = nc.tensor.matmul(bank(u), a[:, g % 2, dc, j, k * P:(k + 1) * P], xx[:, dc, cols],
                                            start=(i == 0), stop=(i == len(terms) - 1))
                piece_done(u, last)

            def rank_chunk(u, n, k):
                g = n // 2
                pe.wait_ge(ring_free, ready[("m", g, 1)])
                pe.wait_ge(rope_ready, n * PC + k + 1)
                for j in range(2):
                    nc.tensor.matmul(bank(u), m_sb[:, g % 2, j, k, :], roped[:, j, k, :], start=(j == 0), stop=False,
                                     skip_group_check=True)

            def rank_queries(u, n):
                rank_chunk(u, n, 2)
                m = m_sb[:, (n // 2) % 2]
                for j in range(2):
                    first = nc.tensor.matmul(bank(u - 1)[64:128, :], m[0:64, j, 1, 0:64], roped[0:64, j, 1, :],
                                             start=False, stop=(j == 1), skip_group_check=True)
                    second = nc.tensor.matmul(bank(u)[0:64, :], m[64:128, j, 1, 64:128], roped[64:128, j, 1, :],
                                              start=False, stop=(j == 1), skip_group_check=True)
                piece_done(u - 1, first)
                piece_done(u, second)

            def pieces(slot):
                for u, piece in slot:
                    free(u)
                    {"x": turn_x, "k": turn_keys, "a": merge_queries, "m": merge_ranks,
                     "o": lambda u, g, _: merge_outputs(u, g), "q": project, "r": lambda u, n: rank_chunk(u, n, 0), "p": rank_queries}[piece[0]](u, *piece[1:])

            def make_scores(i):
                n, head, b = item_of(i)
                pe.wait_ge(ring_free, ready[("p", n)] - 1 + head // 2)
                if i >= 2:
                    pe.wait_ge(exp_ready, i - 1)
                key = slice(((n % 2) * 2 + b) * L, ((n % 2) * 2 + b + 1) * L)
                for half in range(2):
                    q = q_stack[:, head, b * S + half * P:b * S + (half + 1) * P]
                    nc.tensor.matmul(scores[:, i % 2, half, :], q, keys_hi[:, key], start=True, stop=False)
                    last = nc.tensor.matmul(scores[:, i % 2, half, :], q, keys_lo[:, key], start=False, stop=True)
                last.then_inc(scores_ready, 1)

            def turn_probs(i):
                pe.wait_ge(probs_ready, i + 1)
                if i:
                    pe.wait_ge(probs_t_ready, i)
                for kc in range(2):
                    for half in range(2):
                        last = nc.tensor.transpose(probs_t[:, kc, half * P:(half + 1) * P],
                                                   probs[:, i % E_BUFS, half, kc * P:(kc + 1) * P], ident[:])
                last.then_inc(transposed, 1)

            def make_context(q):
                n, head, b = item_of(2 * q)
                pe.wait_ge(probs_t_ready, 2 * q + 2)
                if q:
                    pe.wait_ge(context_copied, q)
                for kc in range(2):
                    for e in range(2):
                        last = nc.tensor.matmul(context[64 * e:64 * e + 64, 0:S],
                                                keys[:, ((n % 2) * 2 + b) * 2 + kc, 0, :],
                                                probs_t_sb[:, (2 * q + e) % T_BUFS, kc, :],
                                                start=(kc == 0), stop=(kc == 1))
                last.then_inc(context_ready, 1)

            pe.wait_ge(filled, 4)
            pieces(before)
            for i in range(LEAD):
                make_scores(i)
            for n in range(STEPS):
                for s in range(ITEMS):
                    i = n * ITEMS + s
                    if i >= 3 and i % 2 == 1:
                        make_context(i // 2 - 1)
                    if i + LEAD < items and s != 6:
                        make_scores(i + LEAD)
                    pieces(steps[n][s])
                    if i + LEAD < items and s == 6:
                        make_scores(i + LEAD)
                    turn_probs(i)
            make_context(items // 2 - 1)

            def wait_tail(pe, u):
                before_use = u - RING
                if before_use < n_ring:
                    pe.wait_ge(ring_free, before_use + 1)
                    return
                for c in range(CHUNKS):
                    if out_use(c) == before_use:
                        pe.wait_ge(x1_ready, c + 1)
                    if acc_use(c) == before_use:
                        pe.wait_ge(y_ready, c + 1)

            pe.wait_ge(ffn_in, 48)
            for slot in range(CHUNKS + 5):
                c = slot - 4
                if 0 <= c < CHUNKS:
                    u = acc_use(c)
                    wait_tail(pe, u)
                    pe.wait_ge(taken_t_ready, c + 1)
                    nc.tensor.matmul(bank(u)[:, 0:D], taken_t[:, c % 2, :], expert_b_sb[:], start=True, stop=True
                                     ).then_inc(ring_full, 1)
                c = slot - 3
                if 0 <= c < CHUNKS:
                    pe.wait_ge(taken_ready, c + 1)
                    if c == 0:
                        pe.wait_ge(context_copied, items // 2)
                    else:
                        pe.wait_ge(taken_t_ready, c)
                    nc.tensor.transpose(context[0:E, 0:P], taken[:, c % 2, :], ident[:]).then_inc(taken_turned, 1)
                c = slot - 2
                if 0 <= c < CHUNKS:
                    pe.wait_ge(xn2_t_ready, c + 1)
                    if c:
                        pe.wait_ge(exp2_ready, c)
                    nc.tensor.matmul(probs_t[:, 0, 0:E], ones[:], router_b_sb[:], start=True, stop=False)
                    for dc in range(2):
                        last = nc.tensor.matmul(probs_t[:, 0, 0:E], xn2_t[:, c % 2, dc, :], router_t_sb[:, dc, :],
                                                start=False, stop=(dc == 1))
                    last.then_inc(logits_ready, 1)
                c = slot
                if c < CHUNKS:
                    u = out_use(c)
                    wait_tail(pe, u)
                    if c == 0:
                        pe.wait_ge(context_copied, items // 2)
                    for pair in range(PAIRS):
                        last = nc.tensor.matmul(bank(u)[:, 0:D], context_t[:, pair, c * P:(c + 1) * P],
                                                o_sb[:, pair, :], start=(pair == 0), stop=(pair == PAIRS - 1))
                    last.then_inc(ring_full, 1)
                c = slot - 1
                if 0 <= c < CHUNKS:
                    pe.wait_ge(xn2_ready, c + 1)
                    if c >= 2:
                        pe.wait_ge(xn2_t_ready, c - 1)
                    for dc in range(2):
                        last = nc.tensor.transpose(scores[:, c % 2, 0, dc * P:(dc + 1) * P],
                                                   xn2[:, c, dc * P:(dc + 1) * P], ident[:])
                    last.then_inc(xn2_turned, 1)


def rope_rows(length, dim):
    inv = np.float32(1.0) / np.float32(10000.0) ** (np.arange(0, dim, 2, dtype=np.float32) / np.float32(dim))
    f = np.arange(length, dtype=np.float32)[:, None] * inv[None, :].astype(np.float32)
    return np.repeat(np.sin(f), 2, axis=-1).astype(np.float32), np.repeat(np.cos(f), 2, axis=-1).astype(np.float32)


def rope_tables():
    sin, cos = rope_rows(S, CQ)
    q = np.zeros((P, PC, 4, S), np.float32)
    for k in range(PC):
        c = (k * P + np.arange(P)) % HALF
        q[:, k, 0], q[:, k, 1] = cos[:, c].T, -sin[:, c].T
        q[:, k, 2], q[:, k, 3] = cos[:, c + HALF].T, sin[:, c + HALF].T
    sin, cos = rope_rows(L, DC)
    sin = np.concatenate([-sin[:, :DC // 2], sin[:, DC // 2:]], axis=1)
    k = np.stack([cos, sin], axis=1).reshape(2, P, 2, DC).transpose(1, 0, 2, 3)
    return q, np.ascontiguousarray(k)


def lay_out(inputs):
    w_qr, w_kr = np.asarray(inputs["L0_xattn_W_qr"]), np.asarray(inputs["L0_xattn_W_kr"])
    qr = np.zeros((GROUPS, 2, R, 2, PC, P), np.float32)
    kr = np.zeros((GROUPS, 2, R, PC, 2, DC), np.float32)
    for g in range(GROUPS):
        for k in range(PC):
            for p in range(P):
                hh, c = divmod(k * P + p, HALF)
                for j in range(2):
                    qr[g, hh - k, :, j, k, p] = w_qr[g * GH + hh, c + HALF * j, :]
            for slot in range(2):
                kr[g, slot, :, k, slot, :] = w_kr[g * GH + k + slot].T
    rope_q, rope_k = rope_tables()
    c = np.ascontiguousarray
    return {
        "x": c(np.asarray(inputs["x"]).reshape(TOKENS, D)),
        "ctx": c(np.asarray(inputs["ctx_512"]).reshape(B * L, DC)),
        "gate_attn": c(inputs["g_xattn"]),
        "gate_ffn": c(inputs["g_ffn"]),
        "wq": c(np.asarray(inputs["L0_xattn_Wq"]).reshape(H, K, D)),
        "w_kc_q": c(inputs["L0_xattn_w_kc_q"]),
        "w_kc_kv": c(inputs["L0_xattn_w_kc_kv"]),
        "w_qr": qr.reshape(GROUPS, P, 2, PC, P),
        "w_kr": kr.reshape(GROUPS, P, PC, P),
        "wo_t": c(np.asarray(inputs["L0_xattn_Wo"]).T.reshape(H, K, D)),
        "router_t": c(np.asarray(inputs["L0_ffn_router_weight"]).T),
        "router_b": c(inputs["L0_ffn_router_bias"]),
        "expert_b": c(inputs["L0_ffn_expert_bias"]),
        "rope_q": rope_q,
        "rope_k": rope_k,
    }


def kernel(**inputs):
    import concourse.bacc as bacc
    from concourse.bass_utils import run_bass_kernel_spmd

    arrays = lay_out(inputs)
    nc = bacc.Bacc("TRN2", target_bir_lowering=False, num_devices=1)
    args = [nc.dram_tensor(f"in_{n}", a.shape, mybir.dt.from_np(a.dtype), kind="ExternalInput").ap()
            for n, a in arrays.items()]
    out = nc.dram_tensor("out", (TOKENS, D), F32, kind="ExternalOutput").ap()
    flamingo_gated_layer(nc, *args, out)
    r = run_bass_kernel_spmd(nc, [{f"in_{n}": a for n, a in arrays.items()}], core_ids=[0])
    return r.results[0]["out"].reshape(B, S, D)
```

```python
from contextlib import ExitStack

import numpy as np

import concourse.bass as bass
from concourse import mybir

P = 128
F32 = mybir.dt.float32
F32R = mybir.dt.float32r
ALU = mybir.AluOpType
ACT = mybir.ActivationFunctionType
AX_X = mybir.AxisListType.X

B, S, D = 4, 256, 256
L, DC = 256, 64
H, K, CQ, R = 16, 128, 192, 64
E, TOP = 64, 8
EPS = 1e-5
TOKENS = B * S
CHUNKS = TOKENS // P

HALF = CQ // 2
GH = 4
GROUPS = H // GH
PC = GH * HALF // P
SPAN = 512
STEPS = GROUPS * TOKENS // SPAN
ITEMS = GH * 2
RING = 4
E_BUFS, T_BUFS = 4, 4
WARM_UP = 40
LEAD = 2


NO_BANK = ("n", "c", "norm", "take", "part")
FREED_BY_SCALAR = ("m", "turn", "logit", "pick")
SPLIT = ("x", "k", "a", "o", "p")


def weights(g):
    return [("a", g, hh) for hh in range(GH)] + [("m", g, 0), ("m", g, 1), ("o", g, 0)]


def queries(n):
    return [("q", n, k, j) for k in range(PC) for j in range(2)]


def pieces_before():
    w, q = weights(0), queries(0)
    return [("n", 0), ("n", 1), w[0], w[1], ("x", 0, 0), w[2], ("c",), ("x", 0, 1), w[3], w[4], q[0], q[1],
            q[2], q[3], q[4], q[5], ("k", 0), w[5], ("k", 1), ("r", 0), ("n", 2), ("n", 3), ("p", 0),
            ("x", 1, 0), ("x", 1, 1), w[6]]


def pieces_of_step(n):
    w, q, r, p = weights(n // 2 + 1), queries(n + 1), ("r", n + 1), ("p", n + 1)
    first_out = ("out", n, n % 2 * 4, 2)
    second_out = ("out", n - 1, (n - 1) % 2 * 4 + 2, 2)
    if n == 0:
        slots = [
            ([q[0]], [q[1], q[2]]),
            ([q[3]], [q[4]]),
            ([], []),
            ([w[0], q[5]], []),
            ([w[1]], [w[2]]),
            ([r, p, w[3]], []),
            ([w[6]], [first_out]),
            ([w[4], w[5]], []),
        ]
    elif n == STEPS - 1:
        slots = [
            ([("norm", 0, 2)], []),
            ([], [("turn", 0, 2)]),
            ([second_out, ("logit", 0, 2), ("norm", 2, 2), ("take", 0, 2)], []),
            ([], []),
            ([("part", 0, 2), ("pick", 0, 2)], []),
            ([("mix", 0, 2)], [("turn", 2, 2)]),
            ([("out", STEPS - 1, 4, 2)], [("logit", 2, 2)]),
            ([], [("take", 2, 2), ("norm", 4, 2)]),
        ]
    elif n == STEPS - 2:
        slots = [
            ([q[0], q[1], q[2], q[3]], []),
            ([], [q[4]]),
            ([q[5]], []),
            ([], [second_out]),
            ([r], []),
            ([p], []),
            ([], []),
            ([first_out], []),
        ]
    elif n % 2:
        slots = [
            ([q[0], q[1]], [q[2]]),
            ([], []),
            ([q[3], q[4]], []),
            ([q[5], second_out], [r]),
            ([], []),
            ([p, first_out], []),
            ([], []),
            ([], []),
        ]
    else:
        slots = [
            ([q[0]], [q[1], q[2]]),
            ([q[3]], [q[4], second_out]),
            ([], []),
            ([w[0], q[5]], []),
            ([w[1]], [w[2]]),
            ([r, p, w[3]], []),
            ([w[6]], [first_out]),
            ([w[4], w[5]], []),
        ]
    return slots


def pieces_after():
    return [("out", STEPS - 1, 6, 1), ("pick", 2, 2), ("out", STEPS - 1, 7, 1), ("turn", 4, 2),
            ("norm", 6, 1), ("part", 2, 2), ("logit", 4, 2), ("norm", 7, 1), ("mix", 2, 2), ("turn", 6, 1),
            ("take", 4, 2), ("turn", 7, 1), ("logit", 6, 1), ("logit", 7, 1), ("take", 6, 1),
            ("take", 7, 1), ("pick", 4, 2), ("pick", 6, 1), ("part", 4, 2), ("part", 6, 1), ("pick", 7, 1),
            ("mix", 4, 2), ("mix", 6, 1), ("part", 7, 1), ("mix", 7, 1)]


def ring_plan():
    return pieces_before(), [pieces_of_step(n) for n in range(STEPS)], pieces_after()


def number(before, steps, after):
    used = 0

    def take(pieces):
        nonlocal used
        out = []
        for piece in pieces:
            out.append((used, piece))
            used += piece[0] not in NO_BANK
        return out

    before = take(before)
    steps = [[(take(early), take(late)) for early, late in slots] for slots in steps]
    return before, steps, take(after)


def flamingo_gated_layer(nc, x, ctx, gate_attn, gate_ffn, wq, w_kc_q, w_kc_kv, w_qr, w_kr, wo_t,
                         router_t, router_b, expert_b, rope_q, rope_k, out):
    before, steps, after = number(*ring_plan())
    items = STEPS * ITEMS

    everything = before + [q for slots in steps for slot in slots for part in slot for q in part] + after
    banks = [piece for _, piece in everything if piece[0] not in NO_BANK]
    assert all(banks[banks.index(("p", n)) - 1] == ("r", n) for n in range(STEPS))

    hi_count, count = {}, 0
    for _, piece in everything:
        if piece[0] in SPLIT:
            hi_count[piece] = count + 1
            count += 2 if piece[0] == "p" else 1

    with ExitStack() as stack:
        def sb(name, shape, dt=F32):
            return stack.enter_context(nc.sbuf_tensor(name, shape, dt))

        def psum(name, shape):
            return stack.enter_context(nc.psum_tensor(name, shape, F32))

        def sem(name):
            return stack.enter_context(nc.semaphore(name))

        ring = psum("ring", [P, RING, 512])
        scores = psum("scores", [P, 2, 2, L])
        probs_t = psum("probs_t", [P, 2, S])
        context = psum("context", [P, 512])

        x_sb = sb("x_sb", [P, CHUNKS, D])
        ctx_sb = sb("ctx_sb", [P, CHUNKS, DC])
        gates = sb("gates", [P, 2])
        rope_q_sb = sb("rope_q_sb", [P, PC, 4, S])
        rope_k_sb = sb("rope_k_sb", [P, 2, 2, DC])
        wq_sb = sb("wq_sb", [P, GH, D])
        w_kc_q_sb = sb("w_kc_q_sb", [P, GH, CQ])
        w_kc_kv_sb = sb("w_kc_kv_sb", [P, GH, DC])
        wo_t_sb = sb("wo_t_sb", [P, GH, D])
        w_qr_sb = sb("w_qr_sb", [P, 2, PC, P])
        w_kr_sb = sb("w_kr_sb", [P, PC, P])
        router_t_sb = sb("router_t_sb", [P, 2, E])
        router_b_sb = sb("router_b_sb", [1, E])
        expert_b_sb = sb("expert_b_sb", [E, D])

        ident = sb("ident", [P, P])
        ones = sb("ones", [1, P])
        warm = sb("warm", [P, 1])
        tanh_gates = sb("tanh_gates", [P, 2])
        stats = sb("stats", [P, CHUNKS, 6])
        moments = sb("moments", [P, CHUNKS, 2])
        var_eps = sb("var_eps", [P, CHUNKS])
        rstd = sb("rstd", [P, CHUNKS])
        minus_half = sb("minus_half", [P, 2])
        neg_max = sb("neg_max", [P, 4, 2])
        row_sum = sb("row_sum", [P, 4, 2])
        inv_sum = sb("inv_sum", [P, 4, 2])

        xn_hi = sb("xn_hi", [P, 2, TOKENS], F32R)
        xn_lo = sb("xn_lo", [P, 2, TOKENS], F32R)
        a_hi = sb("a_hi", [P, 2, 2, 2, GH * HALF], F32R)
        a_lo = sb("a_lo", [P, 2, 2, 2, GH * HALF], F32R)
        keys_hi = sb("keys_hi", [P, B * L], F32R)
        keys_lo = sb("keys_lo", [P, B * L], F32R)
        q_stack = sb("q_stack", [P, GH, SPAN], F32R)

        o_hi = sb("o_hi", [P, 2, 2, D], F32R)
        o_lo = sb("o_lo", [P, 2, 2, D], F32R)
        context_hi = sb("context_hi", [P, 2, 2, SPAN], F32R)
        context_lo = sb("context_lo", [P, 2, 2, SPAN], F32R)

        keys = sb("keys", [P, CHUNKS, 2, DC])
        m_sb = sb("m_sb", [P, 2, 2, PC, P])
        roped = sb("roped", [P, 2, PC, SPAN])
        cross = sb("cross", [P, 2, 2, SPAN])
        probs = sb("probs", [P, E_BUFS, 2, L])
        probs_t_sb = sb("probs_t_sb", [P, T_BUFS, 2, S])
        xn = probs_t_sb[:, :, :, :].rearrange("p a b d -> p (a b) d")

        xn2 = roped[:, :, :, :].rearrange("p a b c -> p (a b c)")[:, 0:TOKENS * D // P].rearrange(
            "p (c d) -> p c d", d=D)
        xn2_t = sb("xn2_t", [P, 4, 2, P])
        expo = sb("expo", [P, CHUNKS, E])
        rest = sb("rest", [P, CHUNKS, E])
        taken = sb("taken", [P, CHUNKS, E])
        taken_t = sb("taken_t", [E, 4, P])
        neg_max2 = sb("neg_max2", [P, CHUNKS])
        sum2 = sb("sum2", [P, CHUNKS])
        inv2 = sb("inv2", [P, CHUNKS])
        top8 = sb("top8", [P, CHUNKS, TOP])
        top_sum = sb("top_sum", [P, CHUNKS])
        scale_e = sb("scale_e", [P, CHUNKS])
        scale_x = sb("scale_x", [P, CHUNKS])

        x_in = [sem(f"x_in{i}") for i in range(4)]
        ctx_in = sem("ctx_in")
        rope_k_in = sem("rope_k_in")
        rope_q_in = sem("rope_q_in")
        gates_in = sem("gates_in")
        ffn_in = sem("ffn_in")
        wq_in = [sem(f"wq_in{g}") for g in range(GROUPS)]
        wr_in = [sem(f"wr_in{g}") for g in range(GROUPS)]
        wo_in = [sem(f"wo_in{g}") for g in range(GROUPS)]
        stored = sem("stored")
        filled = sem("filled")
        warmed = sem("warmed")
        gated = sem("gated")
        stats_ready = sem("stats_ready")
        moments_ready = sem("moments_ready")
        var_ready = sem("var_ready")
        rstd_ready = sem("rstd_ready")
        xn_ready = sem("xn_ready")
        key_products = sem("key_products")
        keys_ready = sem("keys_ready")
        ring_full = sem("ring_full")
        ring_free = sem("ring_free")
        ring_copied = sem("ring_copied")
        hi_ready = sem("hi_ready")
        rope_ready = sem("rope_ready")
        scores_ready = sem("scores_ready")
        max_ready = sem("max_ready")
        exp_ready = sem("exp_ready")
        inv_ready = sem("inv_ready")
        probs_ready = sem("probs_ready")
        transposed = sem("transposed")
        probs_t_ready = sem("probs_t_ready")
        context_ready = sem("context_ready")
        context_hi_ready = sem("context_hi_ready")
        context_lo_ready = sem("context_lo_ready")
        stats2_ready = sem("stats2_ready")
        moments2_ready = sem("moments2_ready")
        var2_ready = sem("var2_ready")
        rstd2_ready = sem("rstd2_ready")
        xn2_ready = sem("xn2_ready")
        max2_ready = sem("max2_ready")
        top_ready = sem("top_ready")
        rest_ready = sem("rest_ready")
        taken_ready = sem("taken_ready")
        inv2_ready = sem("inv2_ready")
        top_sum_ready = sem("top_sum_ready")
        scale_e_ready = sem("scale_e_ready")
        scale_x_ready = sem("scale_x_ready")
        partial = sem("partial")

        def bank(u):
            return ring[:, u % RING, :]

        def item_of(i):
            n, s = divmod(i, ITEMS)
            b, pair = s // 4, s // 2 % 2
            return n, 2 * pair + s % 2, b

        by_scalar = [piece[0] in FREED_BY_SCALAR for piece in banks]
        freed = [sum(1 for other in by_scalar[:u + 1] if other == by_scalar[u]) for u in range(len(banks))]
        freed_by = {piece: freed[u] for u, piece in enumerate(banks)}
        stores = [(piece[1], piece[2]) for piece in banks if piece[0] == "mix"]

        weights_end = [
            1 + max(u for u, p in everything if p[0] in ("a", "m", "o") and p[1] == g)
            for g in range(GROUPS)
        ]

        def load_x(queue, i):
            x_dram = x.rearrange("(c p) d -> p c d", p=P)
            queue.dma_start(x_sb[:, 2 * i:2 * i + 2, :], x_dram[:, 2 * i:2 * i + 2, :]).then_inc(x_in[i], 16)

        def load_other_weights(queue, g):
            heads = slice(g * GH, (g + 1) * GH)
            queue.dma_start(w_kc_q_sb[:], w_kc_q[heads].rearrange("h k c -> k h c")).then_inc(wq_in[g], 16)
            queue.dma_start(w_qr_sb[:], w_qr[g]).then_inc(wr_in[g], 16)
            queue.dma_start(w_kr_sb[:], w_kr[g]).then_inc(wr_in[g], 16)
            queue.dma_start(w_kc_kv_sb[:], w_kc_kv[heads].rearrange("h k d -> k h d")).then_inc(wo_in[g], 16)
            queue.dma_start(wo_t_sb[:], wo_t[heads].rearrange("h k d -> k h d")).then_inc(wo_in[g], 16)

        block = stack.enter_context(nc.Block())

        @block.sync
        def _(sp):
            load_x(sp, 0)
            load_x(sp, 1)
            for g in range(GROUPS):
                if g:
                    sp.wait_ge(ring_full, weights_end[g - 1])
                heads = slice(g * GH, (g + 1) * GH)
                sp.dma_start(wq_sb[:], wq[heads].rearrange("h k d -> k h d")).then_inc(wq_in[g], 16)
                if g:
                    load_other_weights(sp, g)
                else:
                    sp.dma_start(ctx_sb[:], ctx.rearrange("(c p) d -> p c d", p=P)).then_inc(ctx_in, 16)
                    sp.dma_start(rope_k_sb[:], rope_k).then_inc(rope_k_in, 16)
                    sp.dma_start(w_qr_sb[:], w_qr[0]).then_inc(wr_in[0], 16)
                    sp.dma_start(w_kr_sb[:], w_kr[0]).then_inc(wr_in[0], 16)
                    sp.dma_start(rope_q_sb[:], rope_q).then_inc(rope_q_in, 16)
                    load_x(sp, 2)
                    load_x(sp, 3)
                    for i, gate in enumerate((gate_attn, gate_ffn)):
                        gate = gate.rearrange("(o a) -> o a", o=1).broadcast_to([P, 1])
                        sp.dma_start(gates[:, i:i + 1], gate).then_inc(gates_in, 16)
                    sp.dma_start(w_kc_kv_sb[:], w_kc_kv[heads].rearrange("h k d -> k h d")).then_inc(wo_in[0], 16)
                    sp.dma_start(wo_t_sb[:], wo_t[heads].rearrange("h k d -> k h d")).then_inc(wo_in[0], 16)
                    sp.dma_start(router_t_sb[:], router_t.rearrange("(c p) e -> p c e", p=P)).then_inc(ffn_in, 16)
                    sp.dma_start(router_b_sb[:], router_b.rearrange("(o e) -> o e", o=1)).then_inc(ffn_in, 16)
                    sp.dma_start(expert_b_sb[:], expert_b).then_inc(ffn_in, 16)
            out_dram = out.rearrange("(c p) d -> p c d", p=P)
            for c, w in stores:
                sp.wait_ge(ring_free, freed_by[("mix", c, w)])
                sp.dma_start(out_dram[:, c:c + w, :], x_sb[:, c:c + w, :]).then_inc(stored, 16)
            sp.wait_ge(stored, 16 * len(stores))

        @block.gpsimd
        def _(pool):
            nc.gpsimd.memset(ident[:], 0.0).then_inc(filled, 1)
            nc.gpsimd.memset(ones[:], 1.0).then_inc(filled, 1)
            nc.gpsimd.memset(minus_half[:], -0.5).then_inc(filled, 1)
            pool.wait_ge(filled, 3)
            nc.gpsimd.affine_select(out=ident[:], in_=ident[:], compare_op=ALU.not_equal, fill=1.0, base=0,
                                    pattern=[[-1, P]], channel_multiplier=1).then_inc(filled, 1)

            def rope_context():
                pool.wait_ge(ctx_in, 16)
                pool.wait_ge(rope_k_in, 16)
                hk = DC // 2
                for b in range(B):
                    c = slice(2 * b, 2 * b + 2)
                    nc.gpsimd.tensor_tensor(keys[:, c, 0, :], ctx_sb[:, c, :], rope_k_sb[:, :, 0, :], ALU.mult)
                    nc.gpsimd.tensor_tensor(keys[:, c, 1, 0:hk], ctx_sb[:, c, hk:DC], rope_k_sb[:, :, 1, 0:hk], ALU.mult)
                    last = nc.gpsimd.tensor_tensor(keys[:, c, 1, hk:DC], ctx_sb[:, c, 0:hk], rope_k_sb[:, :, 1, hk:DC],
                                                   ALU.mult)
                last.then_inc(key_products, 1)
                pool.wait_ge(key_products, 1)
                nc.gpsimd.tensor_tensor(keys[:, :, 0, :], keys[:, :, 0, :], keys[:, :, 1, :], ALU.add
                                        ).then_inc(key_products, 1)
                pool.wait_ge(key_products, 2)
                nc.gpsimd.tensor_copy(keys[:, :, 1, :], keys[:, :, 0, :]).then_inc(keys_ready, 1)

            def rope_sums(n, k, u):
                done = n * PC + k
                pool.wait_ge(ring_free, freed[u])
                for j in range(2):
                    last = nc.gpsimd.tensor_tensor(roped[:, j, k, :], roped[:, j, k, :],
                                                   cross[:, done % 2, j, :], ALU.add)
                last.then_inc(rope_ready, 1)

            def pieces(slot):
                for u, piece in slot:
                    if piece[0] == "c":
                        rope_context()
                    if piece[0] == "n":
                        i = piece[1]
                        pool.wait_ge(var_ready, 2 * i + 2)
                        nc.gpsimd.tensor_tensor(rstd[:, 2 * i:2 * i + 2], var_eps[:, 2 * i:2 * i + 2],
                                                minus_half[:, 0:2], ALU.pow).then_inc(rstd_ready, 2)
                    if piece[0] == "q" and piece[3] == 1:
                        rope_sums(piece[1], piece[2], u)
                    if piece[0] == "norm":
                        second_root(*piece[1:])

            def second_root(c, w):
                pool.wait_ge(var2_ready, c + w)
                nc.gpsimd.tensor_tensor(rstd[:, c:c + w], var_eps[:, c:c + w], minus_half[:, 0:w], ALU.pow
                                        ).then_inc(rstd2_ready, w)

            def normalise(i):
                pool.wait_ge(inv_ready, i + 1)
                for half in range(2):
                    e = probs[:, i % E_BUFS, half, :]
                    last = nc.gpsimd.tensor_scalar(e, e, inv_sum[:, i % 4, half:half + 1], 1.0,
                                                   ALU.mult, ALU.mult)
                last.then_inc(probs_ready, 1)

            pieces(before)
            normalise(0)
            for n in range(STEPS):
                for s in range(ITEMS):
                    if n * ITEMS + s + 1 < items:
                        normalise(n * ITEMS + s + 1)
                    pieces(steps[n][s][0])
                    pieces(steps[n][s][1])
            pieces(after)

        @block.scalar
        def _(act):
            heads = slice(0, GH)
            act.dma_start(w_kc_q_sb[:], w_kc_q[heads].rearrange("h k c -> k h c")).then_inc(wq_in[0], 16)

            def pieces(slot):
                for u, piece in slot:
                    kind = piece[0]
                    if kind == "logit":
                        exponentials2(u, *piece[1:])
                    elif kind == "turn":
                        _, c, w = piece
                        act.wait_ge(ring_full, u + 1)
                        nc.scalar.copy(xn2_t[:, c % 4:c % 4 + w].rearrange("p a d t -> p (a d t)"),
                                       bank(u)[:, 0:w * 2 * P]).then_inc(ring_copied, 1)
                    elif kind == "m":
                        _, g, j = piece
                        act.wait_ge(ring_full, u + 1)
                        nc.scalar.copy(m_sb[:, g % 2, j, :, :],
                                       bank(u)[:, 0:PC * P].rearrange("p (k c) -> p k c", k=PC)).then_inc(ring_copied, 1)
                    elif kind == "pick":
                        _, c, w = piece
                        act.wait_ge(ring_full, u + 1)
                        nc.scalar.copy(taken_t[:, c % 4:c % 4 + w].rearrange("p a t -> p (a t)"),
                                       bank(u)[0:E, 0:w * P]).then_inc(ring_copied, 1)
                    if kind not in SPLIT:
                        continue
                    if kind == "p":
                        stack_queries(u, piece[1])
                        continue
                    act.wait_ge(ring_full, u + 1)
                    if kind == "x":
                        _, t, dc = piece
                        nc.scalar.copy(xn_hi[:, dc, t * SPAN:(t + 1) * SPAN], bank(u)).then_inc(hi_ready, 1)
                    elif kind == "k":
                        i = piece[1]
                        nc.scalar.copy(keys_hi[:, i * 512:(i + 1) * 512], bank(u)).then_inc(hi_ready, 1)
                    elif kind == "o":
                        g = piece[1]
                        if g == 0:
                            act.wait_ge(gates_in, 32)
                            nc.scalar.activation(tanh_gates[:], gates[:], ACT.Tanh).then_inc(gated, 1)
                            act.wait_ge(gated, 1)
                        nc.scalar.activation(o_hi[:, g % 2], bank(u).rearrange("p (a d) -> p a d", a=2), ACT.Identity,
                                             scale=tanh_gates[:, 0:1]).then_inc(hi_ready, 1)
                    elif kind == "a":
                        _, g, hh = piece
                        src = bank(u)[:, 0:2 * CQ].rearrange("p (c j r) -> p c j r", c=2, j=2)
                        dst = a_hi[:, g % 2, :, :, hh * HALF:(hh + 1) * HALF]
                        nc.scalar.copy(dst, src).then_inc(hi_ready, 1)

            def exponentials2(u, c, w):
                act.wait_ge(max2_ready, c + w)
                for e in range(w):
                    last = nc.scalar.activation(expo[:, c + e, :], bank(u)[:, e * E:(e + 1) * E], ACT.Exp,
                                                bias=neg_max2[:, c + e:c + e + 1],
                                                accum_out=sum2[:, c + e:c + e + 1])
                last.then_inc(ring_copied, 1)

            def stack_queries(u, n):
                for pair in range(2):
                    act.wait_ge(ring_full, u + pair)
                    if n:
                        act.wait_ge(scores_ready, (n - 1) * ITEMS + ITEMS - 4 + 2 * pair + 2)
                    nc.scalar.copy(q_stack[0:64, 2 * pair, :], bank(u - 1 + pair)[0:64, :])
                    last = nc.scalar.copy(q_stack[64:128, 2 * pair + 1, :], bank(u - 1 + pair)[64:128, :])
                    last.then_inc(hi_ready, 1)

            def exponentials(i):
                act.wait_ge(max_ready, i + 1)
                if i >= E_BUFS:
                    act.wait_ge(transposed, i - E_BUFS + 1)
                for half in range(2):
                    last = nc.scalar.activation(probs[:, i % E_BUFS, half, :], scores[:, i % 2, half, :], ACT.Exp,
                                                bias=neg_max[:, i % 4, half:half + 1],
                                                accum_out=row_sum[:, i % 4, half:half + 1])
                last.then_inc(exp_ready, 1)

            def copy_transposed(i):
                act.wait_ge(transposed, i + 1)
                if i >= T_BUFS:
                    act.wait_ge(context_ready, (i - T_BUFS) // 2 + 1)
                nc.scalar.copy(probs_t_sb[:, i % T_BUFS], probs_t[:]).then_inc(probs_t_ready, 1)

            def copy_context(q):
                n, head, b = item_of(2 * q)
                act.wait_ge(context_ready, q + 1)
                nc.scalar.copy(context_hi[:, n % 2, head // 2, b * S:(b + 1) * S],
                               context[:, 0:S]).then_inc(context_hi_ready, 1)

            act.wait_ge(filled, 4)
            nc.scalar.activation(warm[:], ident[:, 0:1], ACT.Exp).then_inc(warmed, 1)
            pieces(before)
            for i in range(LEAD):
                exponentials(i)
            for n in range(STEPS):
                for s in range(ITEMS):
                    i = n * ITEMS + s
                    if i >= 3 and i % 2 == 1:
                        copy_context(i // 2 - 1)
                    pieces(steps[n][s][0])
                    copy_transposed(i)
                    if i + LEAD < items:
                        exponentials(i + LEAD)
                    pieces(steps[n][s][1])
            copy_context(items // 2 - 1)
            pieces(after)

        @block.vector
        def _(dve):
            def variances(c, w, stats_done, moments_done, var_done):
                for e in range(c, c + w):
                    last = nc.vector.bn_stats(stats[:, e, :], x_sb[:, e, :])
                last.then_inc(stats_done, w)
                dve.wait_ge(stats_done, c + w)
                for e in range(c, c + w):
                    last = nc.vector.bn_aggr(moments[:, e, :], stats[:, e, :])
                last.then_inc(moments_done, w)
                dve.wait_ge(moments_done, c + w)
                nc.vector.tensor_scalar(var_eps[:, c:c + w], moments[:, c:c + w, 1], EPS, None, ALU.add
                                        ).then_inc(var_done, w)

            def normalise(dst, c, w, rstd_done, done):
                dve.wait_ge(rstd_done, c + w)
                for e in range(c, c + w):
                    last = nc.vector.tensor_scalar(dst[:, e, :], x_sb[:, e, :], moments[:, e, 0:1], rstd[:, e:e + 1],
                                                   ALU.subtract, ALU.mult)
                last.then_inc(done, w)

            def layer_norm(i):
                dve.wait_ge(x_in[i], 16)
                variances(2 * i, 2, stats_ready, moments_ready, var_ready)
                normalise(xn, 2 * i, 2, rstd_ready, xn_ready)

            def low(dst, src, hi, piece, extra=0):
                dve.wait_ge(hi_ready, hi_count[piece] + extra)
                return nc.vector.tensor_tensor(dst, src, hi.bitcast(F32), ALU.subtract)

            def rope(n, k, j, u):
                done = n * PC + k
                if j == 0 and done >= 2:
                    dve.wait_ge(rope_ready, done - 1)
                if done == 0 and j == 0:
                    dve.wait_ge(rope_q_in, 16)
                dve.wait_ge(ring_full, u + 1)
                q = bank(u).rearrange("p (b s) -> p b s", b=2)
                straight = rope_q_sb[:, k, 2 * j:2 * j + 1, :].broadcast_to([P, 2, S])
                crossed = rope_q_sb[:, k, 3 - 2 * j:4 - 2 * j, :].broadcast_to([P, 2, S])
                nc.vector.tensor_tensor(roped[:, j, k, :].rearrange("p (b s) -> p b s", b=2), q, straight, ALU.mult)
                last = nc.vector.tensor_tensor(cross[:, done % 2, 1 - j, :].rearrange("p (b s) -> p b s", b=2), q,
                                               crossed, ALU.mult)
                last.then_inc(ring_free, 1)

            def add_attention(u, n, c, w):
                dve.wait_ge(ring_full, u + 1)
                nc.vector.tensor_tensor(x_sb[:, c:c + w, :], bank(u)[:, 0:w * D].rearrange("p (c d) -> p c d", c=w),
                                        x_sb[:, c:c + w, :], ALU.add).then_inc(ring_free, 1)
                if n >= STEPS - 2:
                    dve.wait_ge(ring_free, freed[u])
                    variances(c, w, stats2_ready, moments2_ready, var2_ready)

            def context_low(q):
                n, head, b = item_of(2 * q)
                at = (slice(None), n % 2, head // 2, slice(b * S, (b + 1) * S))
                dve.wait_ge(context_hi_ready, q + 1)
                nc.vector.tensor_tensor(context_lo[at], context[:, 0:S], context_hi[at].bitcast(F32), ALU.subtract
                                        ).then_inc(context_lo_ready, 1)

            def maxima2(u, c, w):
                dve.wait_ge(ring_full, u + 1)
                nc.vector.tensor_reduce(neg_max2[:, c:c + w], bank(u)[:, 0:w * E].rearrange("p (c e) -> p c e", c=w),
                                        AX_X, ALU.max, negate=True).then_inc(max2_ready, w)

            def take_experts(c, w):
                end = c + w
                dve.wait_ge(ring_copied, freed_by[("logit", c, w)])
                for e in range(c, end):
                    last = nc.vector.max(top8[:, e, :], expo[:, e, :])
                last.then_inc(top_ready, w)
                nc.vector.reciprocal(inv2[:, c:end], sum2[:, c:end]).then_inc(inv2_ready, w)
                dve.wait_ge(top_ready, end)
                for e in range(c, end):
                    last = nc.vector.match_replace(out=rest[:, e, :], in_to_replace=top8[:, e, :],
                                                   in_values=expo[:, e, :], imm_value=0.0)
                last.then_inc(rest_ready, w)
                nc.vector.tensor_reduce(top_sum[:, c:end], top8[:, c:end, :], AX_X, ALU.add).then_inc(top_sum_ready, w)
                dve.wait_ge(rest_ready, end)
                nc.vector.tensor_tensor(taken[:, c:end, :], expo[:, c:end, :], rest[:, c:end, :], ALU.subtract
                                        ).then_inc(taken_ready, w)

            def add_normed(c, w):
                end = c + w
                dve.wait_ge(inv2_ready, end)
                nc.vector.tensor_tensor(scale_e[:, c:end], inv2[:, c:end], tanh_gates[:, 1:2].broadcast_to([P, w]),
                                        ALU.mult).then_inc(scale_e_ready, w)
                dve.wait_ge(scale_e_ready, end)
                dve.wait_ge(top_sum_ready, end)
                nc.vector.tensor_tensor(scale_x[:, c:end], scale_e[:, c:end], top_sum[:, c:end], ALU.mult
                                        ).then_inc(scale_x_ready, w)
                dve.wait_ge(scale_x_ready, end)
                for e in range(c, end):
                    last = nc.vector.scalar_tensor_tensor(out=x_sb[:, e, :], in0=xn2[:, e, :],
                                                          scalar=scale_x[:, e:e + 1], in1=x_sb[:, e, :],
                                                          op0=ALU.mult, op1=ALU.add)
                last.then_inc(partial, w)

            def finish(u, c, w):
                dve.wait_ge(ring_full, u + 1)
                dve.wait_ge(partial, c + w)
                for e in range(w):
                    last = nc.vector.scalar_tensor_tensor(out=x_sb[:, c + e, :], in0=bank(u)[:, e * D:(e + 1) * D],
                                                          scalar=scale_e[:, c + e:c + e + 1], in1=x_sb[:, c + e, :],
                                                          op0=ALU.mult, op1=ALU.add)
                last.then_inc(ring_free, 1)

            def pieces(slot):
                for u, piece in slot:
                    kind = piece[0]
                    if kind == "x":
                        _, t, dc = piece
                        cols = slice(t * SPAN, (t + 1) * SPAN)
                        last = low(xn_lo[:, dc, cols], bank(u), xn_hi[:, dc, cols], piece)
                        last.then_inc(ring_free, 1)
                    elif kind == "k":
                        cols = slice(piece[1] * 512, (piece[1] + 1) * 512)
                        low(keys_lo[:, cols], bank(u), keys_hi[:, cols], piece).then_inc(ring_free, 1)
                    elif kind == "a":
                        _, g, hh = piece
                        at = (slice(None), g % 2, slice(None), slice(None), slice(hh * HALF, (hh + 1) * HALF))
                        src = bank(u)[:, 0:2 * CQ].rearrange("p (c j r) -> p c j r", c=2, j=2)
                        low(a_lo[at], src, a_hi[at], piece).then_inc(ring_free, 1)
                    elif kind == "o":
                        g = piece[1]
                        dve.wait_ge(hi_ready, hi_count[piece])
                        nc.vector.scalar_tensor_tensor(out=o_lo[:, g % 2], in0=bank(u).rearrange("p (a d) -> p a d", a=2),
                                                       scalar=tanh_gates[:, 0:1], in1=o_hi[:, g % 2].bitcast(F32),
                                                       op0=ALU.mult, op1=ALU.subtract).then_inc(ring_free, 1)
                    elif kind == "q":
                        _, n, k, j = piece
                        rope(n, k, j, u)
                    elif kind == "n":
                        layer_norm(piece[1])
                    elif kind == "out":
                        add_attention(u, *piece[1:])
                    elif kind == "norm":
                        normalise(xn2, *piece[1:], rstd2_ready, xn2_ready)
                    elif kind == "logit":
                        maxima2(u, *piece[1:])
                    elif kind == "take":
                        take_experts(*piece[1:])
                    elif kind == "part":
                        add_normed(*piece[1:])
                    elif kind == "mix":
                        finish(u, *piece[1:])
                    elif kind == "p":
                        for pair in range(2):
                            h0, h1 = 2 * pair, 2 * pair + 1
                            b = bank(u - 1 + pair)
                            low(q_stack[64:128, h0, :], b[0:64, :], q_stack[0:64, h0, :], piece, pair)
                            low(q_stack[0:64, h1, :], b[64:128, :], q_stack[64:128, h1, :], piece, pair
                                ).then_inc(ring_free, 1)

            def maxima(i):
                dve.wait_ge(scores_ready, i + 1)
                nc.vector.tensor_reduce(neg_max[:, i % 4, :], scores[:, i % 2], AX_X, ALU.max,
                                        negate=True).then_inc(max_ready, 1)

            def inverse(i):
                dve.wait_ge(exp_ready, i + 1)
                nc.vector.reciprocal(inv_sum[:, i % 4, :], row_sum[:, i % 4, :]).then_inc(inv_ready, 1)

            pieces(before)
            for i in range(LEAD):
                maxima(i)
            inverse(0)
            for n in range(STEPS):
                for s in range(ITEMS):
                    i = n * ITEMS + s
                    if i + 1 < items:
                        inverse(i + 1)
                    if i + LEAD < items and s != 6:
                        maxima(i + LEAD)
                    if i >= 3 and i % 2 == 1:
                        context_low(i // 2 - 1)
                    pieces(steps[n][s][0])
                    if i + LEAD < items and s == 6:
                        maxima(i + LEAD)
                    pieces(steps[n][s][1])
            context_low(items // 2 - 1)
            pieces(after)

        @block.tensor
        def _(pe):
            def free(u):
                if u >= RING and by_scalar[u - RING]:
                    pe.wait_ge(ring_copied, freed[u - RING])
                elif u >= RING:
                    pe.wait_ge(ring_free, freed[u - RING])

            def piece_done(u, last):
                last.then_inc(ring_full, 1)

            def turn_x(u, t, dc):
                for i in range(4):
                    c = 4 * t + i
                    pe.wait_ge(xn_ready, c // 2 * 2 + 2)
                    last = nc.tensor.transpose(bank(u)[:, i * P:(i + 1) * P], xn[:, c, dc * P:(dc + 1) * P], ident[:])
                piece_done(u, last)

            def turn_keys(u, i):
                pe.wait_ge(keys_ready, 1)
                for c in range(4):
                    last = nc.tensor.transpose(bank(u)[:, c * P:(c + 1) * P],
                                               keys[:, 4 * i + c].rearrange("p a d -> p (a d)"), ident[:])
                piece_done(u, last)

            def merge_queries(u, g, hh):
                pe.wait_ge(wq_in[g], 32)
                for dc in range(2):
                    last = nc.tensor.matmul(bank(u)[:, dc * CQ:(dc + 1) * CQ], wq_sb[:, hh, dc * P:(dc + 1) * P],
                                            w_kc_q_sb[:, hh, :], start=True, stop=True)
                piece_done(u, last)

            def merge_ranks(u, g, j):
                pe.wait_ge(wr_in[g], 32)
                for k in range(PC):
                    last = nc.tensor.matmul(bank(u)[:, k * P:(k + 1) * P], w_qr_sb[:, j, k, :], w_kr_sb[:, k, :],
                                            start=True, stop=True)
                piece_done(u, last)

            def merge_outputs(u, g, _):
                pe.wait_ge(wo_in[g], 32)
                for pair in range(2):
                    for e in range(2):
                        hh = 2 * pair + e
                        last = nc.tensor.matmul(bank(u)[64 * e:64 * e + 64, pair * D:(pair + 1) * D],
                                                w_kc_kv_sb[:, hh, :], wo_t_sb[:, hh, :], start=True, stop=True)
                piece_done(u, last)

            def project(u, n, k, j):
                g, t = n // 2, n % 2
                pe.wait_ge(ring_free, freed_by[("a", g, GH - 1)])
                pe.wait_ge(ring_free, freed_by[("x", t, 1)])
                cols = slice(t * SPAN, (t + 1) * SPAN)
                terms = [(a, xx, dc) for dc in range(2) for a, xx in ((a_hi, xn_hi), (a_hi, xn_lo), (a_lo, xn_hi))]
                for i, (a, xx, dc) in enumerate(terms):
                    last = nc.tensor.matmul(bank(u), a[:, g % 2, dc, j, k * P:(k + 1) * P], xx[:, dc, cols],
                                            start=(i == 0), stop=(i == len(terms) - 1))
                piece_done(u, last)

            def rank_chunk(u, n, k):
                g = n // 2
                pe.wait_ge(ring_copied, freed_by[("m", g, 1)])
                pe.wait_ge(rope_ready, n * PC + k + 1)
                for j in range(2):
                    nc.tensor.matmul(bank(u), m_sb[:, g % 2, j, k, :], roped[:, j, k, :], start=(j == 0), stop=False,
                                     skip_group_check=True)

            def start_rank_queries(u, n):
                rank_chunk(u, n, 0)

            def rank_queries(u, n):
                rank_chunk(u, n, 2)
                m = m_sb[:, (n // 2) % 2]
                for j in range(2):
                    first = nc.tensor.matmul(bank(u - 1)[64:128, :], m[0:64, j, 1, 0:64], roped[0:64, j, 1, :],
                                             start=False, stop=(j == 1), skip_group_check=True)
                    second = nc.tensor.matmul(bank(u)[0:64, :], m[64:128, j, 1, 64:128], roped[64:128, j, 1, :],
                                              start=False, stop=(j == 1), skip_group_check=True)
                piece_done(u - 1, first)
                piece_done(u, second)

            def attention_out(u, n, c, w):
                pe.wait_ge(context_lo_ready, n * ITEMS // 2 + c // 2 % 2 * 2 + 2)
                pe.wait_ge(ring_free, freed_by[("o", n // 2, 0)])
                terms = [(cc, oo, pair) for pair in range(2)
                         for cc, oo in ((context_hi, o_hi), (context_hi, o_lo), (context_lo, o_hi))]
                for e in range(w):
                    cols = slice((c % 4 + e) * P, (c % 4 + e + 1) * P)
                    for i, (cc, oo, pair) in enumerate(terms):
                        last = nc.tensor.matmul(bank(u)[:, e * D:(e + 1) * D], cc[:, n % 2, pair, cols],
                                                oo[:, n // 2 % 2, pair, :], start=(i == 0),
                                                stop=(i == len(terms) - 1))
                piece_done(u, last)

            def turn_xn2(u, c, w):
                pe.wait_ge(xn2_ready, c + w)
                for e in range(w):
                    for dc in range(2):
                        at = (2 * e + dc) * P
                        last = nc.tensor.transpose(bank(u)[:, at:at + P], xn2[:, c + e, dc * P:(dc + 1) * P],
                                                   ident[:])
                piece_done(u, last)

            def logits(u, c, w):
                if c == 0:
                    pe.wait_ge(ffn_in, 48)
                pe.wait_ge(ring_copied, freed_by[("turn", c, w)])
                for e in range(w):
                    to = bank(u)[:, e * E:(e + 1) * E]
                    nc.tensor.matmul(to, ones[:], router_b_sb[:], start=True, stop=False)
                    for dc in range(2):
                        last = nc.tensor.matmul(to, xn2_t[:, (c + e) % 4, dc, :], router_t_sb[:, dc, :],
                                                start=False, stop=(dc == 1))
                piece_done(u, last)

            def turn_taken(u, c, w):
                pe.wait_ge(taken_ready, c + w)
                for e in range(w):
                    last = nc.tensor.transpose(bank(u)[0:E, e * P:(e + 1) * P], taken[:, c + e, :], ident[:])
                piece_done(u, last)

            def mix_experts(u, c, w):
                pe.wait_ge(ring_copied, freed_by[("pick", c, w)])
                for e in range(w):
                    last = nc.tensor.matmul(bank(u)[:, e * D:(e + 1) * D], taken_t[:, (c + e) % 4, :],
                                            expert_b_sb[:], start=True, stop=True)
                piece_done(u, last)

            def pieces(slot):
                for u, piece in slot:
                    if piece[0] in NO_BANK:
                        continue
                    free(u)
                    {"x": turn_x, "k": turn_keys, "a": merge_queries, "m": merge_ranks, "o": merge_outputs,
                     "q": project, "r": start_rank_queries, "p": rank_queries, "out": attention_out,
                     "turn": turn_xn2, "logit": logits, "pick": turn_taken, "mix": mix_experts}[piece[0]](u, *piece[1:])

            def make_scores(i):
                n, head, b = item_of(i)
                pe.wait_ge(ring_free, freed_by[("p", n)] - 1 + head // 2)
                if i >= 2:
                    pe.wait_ge(exp_ready, i - 1)
                key = slice(((n % 2) * 2 + b) * L, ((n % 2) * 2 + b + 1) * L)
                for half in range(2):
                    q = q_stack[:, head, b * S + half * P:b * S + (half + 1) * P]
                    nc.tensor.matmul(scores[:, i % 2, half, :], q, keys_hi[:, key], start=True, stop=False)
                    last = nc.tensor.matmul(scores[:, i % 2, half, :], q, keys_lo[:, key], start=False, stop=True)
                last.then_inc(scores_ready, 1)

            def turn_probs(i):
                pe.wait_ge(probs_ready, i + 1)
                if i:
                    pe.wait_ge(probs_t_ready, i)
                for kc in range(2):
                    for half in range(2):
                        last = nc.tensor.transpose(probs_t[:, kc, half * P:(half + 1) * P],
                                                   probs[:, i % E_BUFS, half, kc * P:(kc + 1) * P], ident[:])
                last.then_inc(transposed, 1)

            def make_context(q):
                n, head, b = item_of(2 * q)
                pe.wait_ge(probs_t_ready, 2 * q + 2)
                if q:
                    pe.wait_ge(context_lo_ready, q)
                for kc in range(2):
                    for e in range(2):
                        last = nc.tensor.matmul(context[64 * e:64 * e + 64, 0:S],
                                                keys[:, ((n % 2) * 2 + b) * 2 + kc, 0, :],
                                                probs_t_sb[:, (2 * q + e) % T_BUFS, kc, :],
                                                start=(kc == 0), stop=(kc == 1))
                last.then_inc(context_ready, 1)

            pe.wait_ge(filled, 4)
            for _ in range(WARM_UP):
                nc.tensor.transpose(scores[:, 0, 0, 0:P], ident[:], ident[:])
            pieces(before)
            for i in range(LEAD):
                make_scores(i)
            for n in range(STEPS):
                for s in range(ITEMS):
                    i = n * ITEMS + s
                    if i >= 3 and i % 2 == 1:
                        make_context(i // 2 - 1)
                    if i + LEAD < items and s != 6:
                        make_scores(i + LEAD)
                    pieces(steps[n][s][0])
                    if i + LEAD < items and s == 6:
                        make_scores(i + LEAD)
                    turn_probs(i)
                    pieces(steps[n][s][1])
            make_context(items // 2 - 1)

            pieces(after)


def rope_rows(length, dim):
    inv = np.float32(1.0) / np.float32(10000.0) ** (np.arange(0, dim, 2, dtype=np.float32) / np.float32(dim))
    f = np.arange(length, dtype=np.float32)[:, None] * inv[None, :].astype(np.float32)
    return np.repeat(np.sin(f), 2, axis=-1).astype(np.float32), np.repeat(np.cos(f), 2, axis=-1).astype(np.float32)


def rope_tables():
    sin, cos = rope_rows(S, CQ)
    q = np.zeros((P, PC, 4, S), np.float32)
    for k in range(PC):
        c = (k * P + np.arange(P)) % HALF
        q[:, k, 0], q[:, k, 1] = cos[:, c].T, -sin[:, c].T
        q[:, k, 2], q[:, k, 3] = cos[:, c + HALF].T, sin[:, c + HALF].T
    sin, cos = rope_rows(L, DC)
    sin = np.concatenate([-sin[:, :DC // 2], sin[:, DC // 2:]], axis=1)
    k = np.stack([cos, sin], axis=1).reshape(2, P, 2, DC).transpose(1, 0, 2, 3)
    return q, np.ascontiguousarray(k)


def lay_out(inputs):
    w_qr, w_kr = np.asarray(inputs["L0_xattn_W_qr"]), np.asarray(inputs["L0_xattn_W_kr"])
    qr = np.zeros((GROUPS, 2, R, 2, PC, P), np.float32)
    kr = np.zeros((GROUPS, 2, R, PC, 2, DC), np.float32)
    for g in range(GROUPS):
        for k in range(PC):
            for p in range(P):
                hh, c = divmod(k * P + p, HALF)
                for j in range(2):
                    qr[g, hh - k, :, j, k, p] = w_qr[g * GH + hh, c + HALF * j, :]
            for slot in range(2):
                kr[g, slot, :, k, slot, :] = w_kr[g * GH + k + slot].T
    rope_q, rope_k = rope_tables()
    c = np.ascontiguousarray
    return {
        "x": c(np.asarray(inputs["x"]).reshape(TOKENS, D)),
        "ctx": c(np.asarray(inputs["ctx_512"]).reshape(B * L, DC)),
        "gate_attn": c(inputs["g_xattn"]),
        "gate_ffn": c(inputs["g_ffn"]),
        "wq": c(np.asarray(inputs["L0_xattn_Wq"]).reshape(H, K, D)),
        "w_kc_q": c(inputs["L0_xattn_w_kc_q"]),
        "w_kc_kv": c(inputs["L0_xattn_w_kc_kv"]),
        "w_qr": qr.reshape(GROUPS, P, 2, PC, P),
        "w_kr": kr.reshape(GROUPS, P, PC, P),
        "wo_t": c(np.asarray(inputs["L0_xattn_Wo"]).T.reshape(H, K, D)),
        "router_t": c(np.asarray(inputs["L0_ffn_router_weight"]).T),
        "router_b": c(inputs["L0_ffn_router_bias"]),
        "expert_b": c(inputs["L0_ffn_expert_bias"]),
        "rope_q": rope_q,
        "rope_k": rope_k,
    }


def kernel(**inputs):
    import concourse.bacc as bacc
    from concourse.bass_utils import run_bass_kernel_spmd

    arrays = lay_out(inputs)
    nc = bacc.Bacc("TRN2", target_bir_lowering=False, num_devices=1)
    args = [nc.dram_tensor(f"in_{n}", a.shape, mybir.dt.from_np(a.dtype), kind="ExternalInput").ap()
            for n, a in arrays.items()]
    out = nc.dram_tensor("out", (TOKENS, D), F32, kind="ExternalOutput").ap()
    flamingo_gated_layer(nc, *args, out)
    r = run_bass_kernel_spmd(nc, [{f"in_{n}": a for n, a in arrays.items()}], core_ids=[0])
    return r.results[0]["out"].reshape(B, S, D)
```

```python
from contextlib import ExitStack

import numpy as np

import concourse.bass as bass
from concourse import mybir

P = 128
F32 = mybir.dt.float32
F32R = mybir.dt.float32r
ALU = mybir.AluOpType
ACT = mybir.ActivationFunctionType
AX_X = mybir.AxisListType.X

B, S, D = 4, 256, 256
L, DC = 256, 64
H, K, CQ, R = 16, 128, 192, 64
E, TOP = 64, 8
EPS = 1e-5
TOKENS = B * S
CHUNKS = TOKENS // P

HALF = CQ // 2
GH = 4
GROUPS = H // GH
PC = GH * HALF // P
SPAN = 512
STEPS = GROUPS * TOKENS // SPAN
ITEMS = GH * 2
RING = 4
E_BUFS, T_BUFS = 4, 4
SHARED_FROM = 4
WARM_UP = 40
LEAD = 2


NO_BANK = ("n", "c", "norm", "take", "part")
FREED_BY_SCALAR = ("m", "turn", "logit", "pick")
SPLIT = ("x", "k", "a", "o", "p")


def weights(g):
    return [("a", g, hh) for hh in range(GH)] + [("m", g, 0), ("m", g, 1), ("o", g, 0)]


def queries(n):
    return [("q", n, k, j) for k in range(PC) for j in range(2)]


def pieces_before():
    w, q = weights(0), queries(0)
    return [("n", 0), ("n", 1), w[0], ("x", 0, 0), w[1], w[2], ("c",), ("x", 0, 1), w[3], w[4], q[0], q[1],
            q[2], q[3], q[4], q[5], ("k", 0), w[5], ("k", 1), ("n", 2), ("r", 0), ("n", 3), ("p", 0),
            ("x", 1, 0), ("x", 1, 1), ("a", 1, 0)]


def pieces_at_start():
    w, q = weights(1), queries(1)
    return [w[1], q[0], ("o", 0, 0)]


def pieces_of_step(n):
    w, q, r, p = weights(n // 2 + 1), queries(n + 1), ("r", n + 1), ("p", n + 1)
    first_out = ("out", n, n % 2 * 4, 2)
    second_out = ("out", n - 1, (n - 1) % 2 * 4 + 2, 2)
    if n == 0:
        slots = [
            ([q[1]], [q[2]]),
            ([q[3]], []),
            ([q[4]], []),
            ([q[5]], [w[2], r]),
            ([], []),
            ([p], [w[6], w[3], first_out]),
            ([], [w[4]]),
            ([w[5]], []),
        ]
    elif n == STEPS - 1:
        slots = [
            ([], [("norm", 0, 2)]),
            ([], [("turn", 0, 2)]),
            ([second_out, ("logit", 0, 2), ("norm", 2, 2)], [("take", 0, 2)]),
            ([], []),
            ([("pick", 0, 2), ("part", 0, 2)], []),
            ([], [("mix", 0, 2)]),
            ([("turn", 2, 2), ("out", STEPS - 1, 4, 2)], [("logit", 2, 2)]),
            ([("norm", 4, 2), ("take", 2, 2)], []),
        ]
    elif n == STEPS - 2:
        slots = [
            ([q[0], q[1], q[2], q[3]], [q[4]]),
            ([], []),
            ([q[5]], []),
            ([], []),
            ([second_out, r], []),
            ([p], []),
            ([], []),
            ([first_out], []),
        ]
    elif n % 2:
        slots = [
            ([q[0]], [q[1]]),
            ([], [q[2]]),
            ([q[3], q[4]], [q[5], second_out]),
            ([], [r]),
            ([], []),
            ([p], []),
            ([first_out], []),
            ([], []),
        ]
    else:
        slots = [
            ([q[0]], [q[1], q[2]]),
            ([q[3]], [q[4]]),
            ([], []),
            ([second_out], [w[0]]),
            ([q[5], w[1], w[2]], []),
            ([r, p], [w[3], w[6]]),
            ([], [w[4], w[5]]),
            ([], [first_out]),
        ]
    return slots


def pieces_after():
    return [("out", STEPS - 1, 6, 1), ("out", STEPS - 1, 7, 1), ("turn", 4, 2), ("part", 2, 2),
            ("pick", 2, 2), ("logit", 4, 2), ("norm", 6, 1), ("norm", 7, 1), ("mix", 2, 2), ("take", 4, 2),
            ("turn", 6, 1), ("turn", 7, 1), ("logit", 6, 1), ("logit", 7, 1), ("take", 6, 1),
            ("pick", 4, 2), ("part", 4, 2), ("take", 7, 1), ("pick", 6, 1), ("part", 6, 1), ("part", 7, 1),
            ("mix", 4, 2), ("pick", 7, 1), ("mix", 6, 1), ("mix", 7, 1)]


def ring_plan():
    return pieces_before(), pieces_at_start(), [pieces_of_step(n) for n in range(STEPS)], pieces_after()


def number(before, start, steps, after):
    used = 0

    def take(pieces):
        nonlocal used
        out = []
        for piece in pieces:
            out.append((used, piece))
            used += piece[0] not in NO_BANK
        return out

    before, start = take(before), take(start)
    steps = [[(take(early), take(late)) for early, late in slots] for slots in steps]
    return before, start, steps, take(after)


def flamingo_gated_layer(nc, x, ctx, gate_attn, gate_ffn, wq, w_kc_q, w_kc_kv, w_qr, w_kr, wo_t,
                         router_t, router_b, expert_b, rope_q, rope_k, out):
    before, start, steps, after = number(*ring_plan())
    items = STEPS * ITEMS

    everything = before + start + [q for slots in steps for slot in slots for part in slot for q in part] + after
    banks = [piece for _, piece in everything if piece[0] not in NO_BANK]
    assert all(banks[banks.index(("p", n)) - 1] == ("r", n) for n in range(STEPS))

    hi_count, count = {}, 0
    for _, piece in everything:
        if piece[0] in SPLIT:
            hi_count[piece] = count + 1
            count += 2 if piece[0] == "p" else 1

    with ExitStack() as stack:
        def sb(name, shape, dt=F32):
            return stack.enter_context(nc.sbuf_tensor(name, shape, dt))

        def psum(name, shape):
            return stack.enter_context(nc.psum_tensor(name, shape, F32))

        def sem(name):
            return stack.enter_context(nc.semaphore(name))

        ring = psum("ring", [P, RING, 512])
        scores = psum("scores", [P, 2, 2, L])
        probs_t = psum("probs_t", [P, 2, S])
        context = psum("context", [P, 512])

        x_sb = sb("x_sb", [P, CHUNKS, D])
        ctx_sb = sb("ctx_sb", [P, CHUNKS, DC])
        gates = sb("gates", [P, 2])
        rope_q_sb = sb("rope_q_sb", [P, PC, 4, S])
        rope_k_sb = sb("rope_k_sb", [P, 2, 2, DC])
        wq_sb = sb("wq_sb", [P, GH, D])
        w_kc_q_sb = sb("w_kc_q_sb", [P, GH, CQ])
        w_kc_kv_sb = sb("w_kc_kv_sb", [P, GH, DC])
        wo_t_sb = sb("wo_t_sb", [P, GH, D])
        w_qr_sb = sb("w_qr_sb", [P, 2, PC, P])
        w_kr_sb = sb("w_kr_sb", [P, PC, P])
        router_t_sb = sb("router_t_sb", [P, 2, E])
        router_b_sb = sb("router_b_sb", [1, E])
        expert_b_sb = sb("expert_b_sb", [E, D])

        ident = sb("ident", [P, P])
        ones = sb("ones", [1, P])
        warm = sb("warm", [P, 1])
        tanh_gates = sb("tanh_gates", [P, 2])
        stats = sb("stats", [P, CHUNKS, 6])
        moments = sb("moments", [P, CHUNKS, 2])
        var_eps = sb("var_eps", [P, CHUNKS])
        rstd = sb("rstd", [P, CHUNKS])
        minus_half = sb("minus_half", [P, 2])
        neg_max = sb("neg_max", [P, 4, 2])
        row_sum = sb("row_sum", [P, 4, 2])
        inv_sum = sb("inv_sum", [P, 4, 2])

        xn_hi = sb("xn_hi", [P, 2, TOKENS], F32R)
        xn_lo = sb("xn_lo", [P, 2, TOKENS], F32R)
        a_hi = sb("a_hi", [P, 2, 2, 2, GH * HALF], F32R)
        a_lo = sb("a_lo", [P, 2, 2, 2, GH * HALF], F32R)
        keys_hi = sb("keys_hi", [P, B * L], F32R)
        keys_lo = sb("keys_lo", [P, B * L], F32R)
        q_stack = sb("q_stack", [P, GH, SPAN], F32R)

        o_hi = sb("o_hi", [P, 2, 2, D], F32R)
        o_lo = sb("o_lo", [P, 2, 2, D], F32R)
        context_hi = sb("context_hi", [P, 2, 2, SPAN], F32R)
        context_lo = sb("context_lo", [P, 2, 2, SPAN], F32R)

        keys = sb("keys", [P, CHUNKS, 2, DC])
        m_sb = sb("m_sb", [P, 2, 2, PC, P])
        roped = sb("roped", [P, 2, PC, SPAN])
        cross = sb("cross", [P, 2, 2, SPAN])
        probs = sb("probs", [P, E_BUFS, 2, L])
        probs_t_sb = sb("probs_t_sb", [P, T_BUFS, 2, S])
        xn = probs_t_sb[:, :, :, :].rearrange("p a b d -> p (a b) d")

        xn2 = roped[:, :, :, :].rearrange("p a b c -> p (a b c)")[:, 0:TOKENS * D // P].rearrange(
            "p (c d) -> p c d", d=D)
        xn2_t = sb("xn2_t", [P, 4, 2, P])
        expo = sb("expo", [P, CHUNKS, E])
        rest = sb("rest", [P, CHUNKS, E])
        taken = sb("taken", [P, CHUNKS, E])
        taken_t = sb("taken_t", [E, 4, P])
        neg_max2 = sb("neg_max2", [P, CHUNKS])
        sum2 = sb("sum2", [P, CHUNKS])
        inv2 = sb("inv2", [P, CHUNKS])
        top8 = sb("top8", [P, CHUNKS, TOP])
        top_sum = sb("top_sum", [P, CHUNKS])
        scale_e = sb("scale_e", [P, CHUNKS])
        scale_x = sb("scale_x", [P, CHUNKS])

        x_in = [sem(f"x_in{i}") for i in range(4)]
        ctx_in = sem("ctx_in")
        rope_k_in = sem("rope_k_in")
        rope_q_in = sem("rope_q_in")
        gates_in = sem("gates_in")
        ffn_in = sem("ffn_in")
        wq_in = [sem(f"wq_in{g}") for g in range(GROUPS)]
        wr_in = [sem(f"wr_in{g}") for g in range(GROUPS)]
        wo_in = [sem(f"wo_in{g}") for g in range(GROUPS)]
        stored = sem("stored")
        filled = sem("filled")
        warmed = sem("warmed")
        gated = sem("gated")
        stats_ready = sem("stats_ready")
        moments_ready = sem("moments_ready")
        var_ready = sem("var_ready")
        rstd_ready = sem("rstd_ready")
        xn_ready = sem("xn_ready")
        key_products = sem("key_products")
        keys_ready = sem("keys_ready")
        ring_full = sem("ring_full")
        ring_free = sem("ring_free")
        ring_copied = sem("ring_copied")
        hi_ready = sem("hi_ready")
        rope_ready = sem("rope_ready")
        scores_ready = sem("scores_ready")
        max_ready = sem("max_ready")
        exp_ready = sem("exp_ready")
        inv_ready = sem("inv_ready")
        probs_ready = sem("probs_ready")
        transposed = sem("transposed")
        probs_t_ready = sem("probs_t_ready")
        context_ready = sem("context_ready")
        context_hi_ready = sem("context_hi_ready")
        context_lo_ready = sem("context_lo_ready")
        stats2_ready = sem("stats2_ready")
        moments2_ready = sem("moments2_ready")
        var2_ready = sem("var2_ready")
        rstd2_ready = sem("rstd2_ready")
        xn2_ready = sem("xn2_ready")
        max2_ready = sem("max2_ready")
        top_ready = sem("top_ready")
        rest_ready = sem("rest_ready")
        taken_ready = sem("taken_ready")
        inv2_ready = sem("inv2_ready")
        top_sum_ready = sem("top_sum_ready")
        scales_ready = sem("scales_ready")
        scaled = sem("scaled")
        partial = sem("partial")
        shared_partial = sem("shared_partial")

        def bank(u):
            return ring[:, u % RING, :]

        def item_of(i):
            n, s = divmod(i, ITEMS)
            b, pair = s // 4, s // 2 % 2
            return n, 2 * pair + s % 2, b

        def last_item(n, pair=None, batch=None):
            return max(i for i in range(n * ITEMS, (n + 1) * ITEMS)
                       if pair in (None, item_of(i)[1] // 2) and batch in (None, item_of(i)[2]))

        by_scalar = [piece[0] in FREED_BY_SCALAR for piece in banks]
        freed = [sum(1 for other in by_scalar[:u + 1] if other == by_scalar[u]) for u in range(len(banks))]
        freed_by = {piece: freed[u] for u, piece in enumerate(banks)}
        stores = [(piece[1], piece[2]) for piece in banks if piece[0] == "mix"]

        def last_merge(kind, g):
            return 1 + max(u for u, piece in enumerate(banks) if piece[:2] == (kind, g))

        def load_x(queue, i):
            x_dram = x.rearrange("(c p) d -> p c d", p=P)
            queue.dma_start(x_sb[:, 2 * i:2 * i + 2, :], x_dram[:, 2 * i:2 * i + 2, :]).then_inc(x_in[i], 16)

        def load_query_weights(queue, g):
            queue.dma_start(wq_sb[:], wq[g * GH:(g + 1) * GH].rearrange("h k d -> k h d")).then_inc(wq_in[g], 16)

        def load_key_weights(queue, g):
            queue.dma_start(w_kc_q_sb[:], w_kc_q[g * GH:(g + 1) * GH].rearrange("h k c -> k h c")
                            ).then_inc(wq_in[g], 16)

        def load_rank_weights(queue, g):
            queue.dma_start(w_qr_sb[:], w_qr[g]).then_inc(wr_in[g], 16)
            queue.dma_start(w_kr_sb[:], w_kr[g]).then_inc(wr_in[g], 16)

        def load_output_weights(queue, g):
            heads = slice(g * GH, (g + 1) * GH)
            queue.dma_start(w_kc_kv_sb[:], w_kc_kv[heads].rearrange("h k d -> k h d")).then_inc(wo_in[g], 16)
            queue.dma_start(wo_t_sb[:], wo_t[heads].rearrange("h k d -> k h d")).then_inc(wo_in[g], 16)

        block = stack.enter_context(nc.Block())

        @block.sync
        def _(sp):
            load_x(sp, 0)
            load_x(sp, 1)
            load_query_weights(sp, 0)
            sp.dma_start(ctx_sb[:], ctx.rearrange("(c p) d -> p c d", p=P)).then_inc(ctx_in, 16)
            sp.dma_start(rope_k_sb[:], rope_k).then_inc(rope_k_in, 16)
            load_rank_weights(sp, 0)
            sp.dma_start(rope_q_sb[:], rope_q).then_inc(rope_q_in, 16)
            load_x(sp, 2)
            load_x(sp, 3)
            load_output_weights(sp, 0)
            for i, gate in enumerate((gate_attn, gate_ffn)):
                gate = gate.rearrange("(o a) -> o a", o=1).broadcast_to([P, 1])
                sp.dma_start(gates[:, i:i + 1], gate).then_inc(gates_in, 16)
            sp.dma_start(router_t_sb[:], router_t.rearrange("(c p) e -> p c e", p=P)).then_inc(ffn_in, 16)
            sp.dma_start(router_b_sb[:], router_b.rearrange("(o e) -> o e", o=1)).then_inc(ffn_in, 16)
            sp.dma_start(expert_b_sb[:], expert_b).then_inc(ffn_in, 16)
            for g in range(1, GROUPS):
                sp.wait_ge(ring_full, last_merge("a", g - 1))
                load_query_weights(sp, g)
                load_key_weights(sp, g)
                sp.wait_ge(ring_full, last_merge("m", g - 1))
                load_rank_weights(sp, g)
                sp.wait_ge(ring_full, last_merge("o", g - 1))
                load_output_weights(sp, g)
            out_dram = out.rearrange("(c p) d -> p c d", p=P)
            for c, w in stores:
                sp.wait_ge(ring_free, freed_by[("mix", c, w)])
                sp.dma_start(out_dram[:, c:c + w, :], x_sb[:, c:c + w, :]).then_inc(stored, 16)
            sp.wait_ge(stored, 16 * len(stores))

        @block.gpsimd
        def _(pool):
            nc.gpsimd.memset(ident[:], 0.0).then_inc(filled, 1)
            nc.gpsimd.memset(ones[:], 1.0).then_inc(filled, 1)
            nc.gpsimd.memset(minus_half[:], -0.5).then_inc(filled, 1)
            pool.wait_ge(filled, 3)
            nc.gpsimd.affine_select(out=ident[:], in_=ident[:], compare_op=ALU.not_equal, fill=1.0, base=0,
                                    pattern=[[-1, P]], channel_multiplier=1).then_inc(filled, 1)

            def rope_context():
                pool.wait_ge(ctx_in, 16)
                pool.wait_ge(rope_k_in, 16)
                hk = DC // 2
                for b in range(B):
                    c = slice(2 * b, 2 * b + 2)
                    nc.gpsimd.tensor_tensor(keys[:, c, 0, :], ctx_sb[:, c, :], rope_k_sb[:, :, 0, :], ALU.mult)
                    nc.gpsimd.tensor_tensor(keys[:, c, 1, 0:hk], ctx_sb[:, c, hk:DC], rope_k_sb[:, :, 1, 0:hk],
                                            ALU.mult)
                    last = nc.gpsimd.tensor_tensor(keys[:, c, 1, hk:DC], ctx_sb[:, c, 0:hk],
                                                   rope_k_sb[:, :, 1, hk:DC], ALU.mult)
                last.then_inc(key_products, 1)
                pool.wait_ge(key_products, 1)
                nc.gpsimd.tensor_tensor(keys[:, :, 0, :], keys[:, :, 0, :], keys[:, :, 1, :], ALU.add
                                        ).then_inc(key_products, 1)
                pool.wait_ge(key_products, 2)
                nc.gpsimd.tensor_copy(keys[:, :, 1, :], keys[:, :, 0, :]).then_inc(keys_ready, 1)

            def rope_sums(n, k, u):
                done = n * PC + k
                pool.wait_ge(ring_free, freed[u])
                for j in range(2):
                    last = nc.gpsimd.tensor_tensor(roped[:, j, k, :], roped[:, j, k, :],
                                                   cross[:, done % 2, j, :], ALU.add)
                last.then_inc(rope_ready, 1)

            def pieces(slot):
                for u, piece in slot:
                    if piece[0] == "c":
                        rope_context()
                    if piece[0] == "n":
                        i = piece[1]
                        pool.wait_ge(var_ready, 2 * i + 2)
                        nc.gpsimd.tensor_tensor(rstd[:, 2 * i:2 * i + 2], var_eps[:, 2 * i:2 * i + 2],
                                                minus_half[:, 0:2], ALU.pow).then_inc(rstd_ready, 2)
                    if piece[0] == "q" and piece[3] == 1:
                        rope_sums(piece[1], piece[2], u)
                    if piece[0] == "part" and piece[1] >= SHARED_FROM:
                        _, c, w = piece
                        pool.wait_ge(scaled, c + w - SHARED_FROM)
                        nc.gpsimd.tensor_tensor(x_sb[:, c:c + w, :], x_sb[:, c:c + w, :], xn2[:, c:c + w, :], ALU.add
                                                ).then_inc(shared_partial, w)
                    if piece[0] == "norm":
                        second_root(*piece[1:])

            def second_root(c, w):
                pool.wait_ge(var2_ready, c + w)
                nc.gpsimd.tensor_tensor(rstd[:, c:c + w], var_eps[:, c:c + w], minus_half[:, 0:w], ALU.pow
                                        ).then_inc(rstd2_ready, w)

            def normalise(i):
                pool.wait_ge(inv_ready, i + 1)
                for half in range(2):
                    e = probs[:, i % E_BUFS, half, :]
                    last = nc.gpsimd.tensor_scalar(e, e, inv_sum[:, i % 4, half:half + 1], 1.0,
                                                   ALU.mult, ALU.mult)
                last.then_inc(probs_ready, 1)

            pieces(before)
            pieces(start)
            normalise(0)
            for n in range(STEPS):
                for s in range(ITEMS):
                    if n * ITEMS + s + 1 < items:
                        normalise(n * ITEMS + s + 1)
                    pieces(steps[n][s][0])
                    pieces(steps[n][s][1])
            pieces(after)

        @block.scalar
        def _(act):
            load_key_weights(act, 0)

            def pieces(slot):
                for u, piece in slot:
                    kind = piece[0]
                    if kind == "logit":
                        exponentials2(u, *piece[1:])
                    elif kind == "turn":
                        _, c, w = piece
                        act.wait_ge(ring_full, u + 1)
                        nc.scalar.copy(xn2_t[:, c % 4:c % 4 + w].rearrange("p a d t -> p (a d t)"),
                                       bank(u)[:, 0:w * 2 * P]).then_inc(ring_copied, 1)
                    elif kind == "part" and piece[1] >= SHARED_FROM:
                        _, c, w = piece
                        act.wait_ge(scales_ready, c + w)
                        for e in range(c, c + w):
                            last = nc.scalar.activation(xn2[:, e, :], xn2[:, e, :], ACT.Identity,
                                                        scale=scale_x[:, e:e + 1])
                        last.then_inc(scaled, w)
                    elif kind == "m":
                        _, g, j = piece
                        act.wait_ge(ring_full, u + 1)
                        nc.scalar.copy(m_sb[:, g % 2, j, :, :],
                                       bank(u)[:, 0:PC * P].rearrange("p (k c) -> p k c", k=PC)
                                       ).then_inc(ring_copied, 1)
                    elif kind == "pick":
                        _, c, w = piece
                        act.wait_ge(ring_full, u + 1)
                        nc.scalar.copy(taken_t[:, c % 4:c % 4 + w].rearrange("p a t -> p (a t)"),
                                       bank(u)[0:E, 0:w * P]).then_inc(ring_copied, 1)
                    if kind not in SPLIT:
                        continue
                    if kind == "p":
                        stack_queries(u, piece[1])
                        continue
                    act.wait_ge(ring_full, u + 1)
                    if kind == "x":
                        _, t, dc = piece
                        nc.scalar.copy(xn_hi[:, dc, t * SPAN:(t + 1) * SPAN], bank(u)).then_inc(hi_ready, 1)
                    elif kind == "k":
                        i = piece[1]
                        nc.scalar.copy(keys_hi[:, i * 512:(i + 1) * 512], bank(u)).then_inc(hi_ready, 1)
                    elif kind == "o":
                        g = piece[1]
                        if g == 0:
                            act.wait_ge(gates_in, 32)
                            nc.scalar.activation(tanh_gates[:], gates[:], ACT.Tanh).then_inc(gated, 1)
                            act.wait_ge(gated, 1)
                        nc.scalar.activation(o_hi[:, g % 2], bank(u).rearrange("p (a d) -> p a d", a=2), ACT.Identity,
                                             scale=tanh_gates[:, 0:1]).then_inc(hi_ready, 1)
                    elif kind == "a":
                        _, g, hh = piece
                        src = bank(u)[:, 0:2 * CQ].rearrange("p (c j r) -> p c j r", c=2, j=2)
                        dst = a_hi[:, g % 2, :, :, hh * HALF:(hh + 1) * HALF]
                        nc.scalar.copy(dst, src).then_inc(hi_ready, 1)

            def exponentials2(u, c, w):
                act.wait_ge(max2_ready, c + w)
                for e in range(w):
                    last = nc.scalar.activation(expo[:, c + e, :], bank(u)[:, e * E:(e + 1) * E], ACT.Exp,
                                                bias=neg_max2[:, c + e:c + e + 1],
                                                accum_out=sum2[:, c + e:c + e + 1])
                last.then_inc(ring_copied, 1)

            def stack_queries(u, n):
                for pair in range(2):
                    act.wait_ge(ring_full, u + pair)
                    if n:
                        act.wait_ge(scores_ready, last_item(n - 1, pair=pair) + 1)
                    nc.scalar.copy(q_stack[0:64, 2 * pair, :], bank(u - 1 + pair)[0:64, :])
                    last = nc.scalar.copy(q_stack[64:128, 2 * pair + 1, :], bank(u - 1 + pair)[64:128, :])
                    last.then_inc(hi_ready, 1)

            def exponentials(i):
                act.wait_ge(max_ready, i + 1)
                if i >= E_BUFS:
                    act.wait_ge(transposed, i - E_BUFS + 1)
                for half in range(2):
                    last = nc.scalar.activation(probs[:, i % E_BUFS, half, :], scores[:, i % 2, half, :], ACT.Exp,
                                                bias=neg_max[:, i % 4, half:half + 1],
                                                accum_out=row_sum[:, i % 4, half:half + 1])
                last.then_inc(exp_ready, 1)

            def copy_transposed(i):
                act.wait_ge(transposed, i + 1)
                if i >= T_BUFS:
                    act.wait_ge(context_ready, (i - T_BUFS) // 2 + 1)
                nc.scalar.copy(probs_t_sb[:, i % T_BUFS], probs_t[:]).then_inc(probs_t_ready, 1)

            def copy_context(q):
                n, head, b = item_of(2 * q)
                act.wait_ge(context_ready, q + 1)
                nc.scalar.copy(context_hi[:, n % 2, head // 2, b * S:(b + 1) * S],
                               context[:, 0:S]).then_inc(context_hi_ready, 1)

            act.wait_ge(filled, 4)
            nc.scalar.activation(warm[:], ident[:, 0:1], ACT.Exp).then_inc(warmed, 1)
            pieces(before)
            exponentials(0)
            pieces(start)
            exponentials(1)
            for n in range(STEPS):
                for s in range(ITEMS):
                    i = n * ITEMS + s
                    if i >= 3 and i % 2 == 1:
                        copy_context(i // 2 - 1)
                    pieces(steps[n][s][0])
                    copy_transposed(i)
                    if i + LEAD < items:
                        exponentials(i + LEAD)
                    pieces(steps[n][s][1])
            copy_context(items // 2 - 1)
            pieces(after)

        @block.vector
        def _(dve):
            def variances(c, w, stats_done, moments_done, var_done):
                for e in range(c, c + w):
                    last = nc.vector.bn_stats(stats[:, e, :], x_sb[:, e, :])
                last.then_inc(stats_done, w)
                dve.wait_ge(stats_done, c + w)
                for e in range(c, c + w):
                    last = nc.vector.bn_aggr(moments[:, e, :], stats[:, e, :])
                last.then_inc(moments_done, w)
                dve.wait_ge(moments_done, c + w)
                nc.vector.tensor_scalar(var_eps[:, c:c + w], moments[:, c:c + w, 1], EPS, None, ALU.add
                                        ).then_inc(var_done, w)

            def normalise(dst, c, w, rstd_done, done):
                dve.wait_ge(rstd_done, c + w)
                for e in range(c, c + w):
                    last = nc.vector.tensor_scalar(dst[:, e, :], x_sb[:, e, :], moments[:, e, 0:1], rstd[:, e:e + 1],
                                                   ALU.subtract, ALU.mult)
                last.then_inc(done, w)

            def layer_norm(i):
                dve.wait_ge(x_in[i], 16)
                variances(2 * i, 2, stats_ready, moments_ready, var_ready)
                normalise(xn, 2 * i, 2, rstd_ready, xn_ready)

            def low(dst, src, hi, piece, extra=0):
                dve.wait_ge(hi_ready, hi_count[piece] + extra)
                return nc.vector.tensor_tensor(dst, src, hi.bitcast(F32), ALU.subtract)

            def rope(n, k, j, u):
                done = n * PC + k
                if j == 0 and done >= 2:
                    dve.wait_ge(rope_ready, done - 1)
                if done == 0 and j == 0:
                    dve.wait_ge(rope_q_in, 16)
                dve.wait_ge(ring_full, u + 1)
                q = bank(u).rearrange("p (b s) -> p b s", b=2)
                straight = rope_q_sb[:, k, 2 * j:2 * j + 1, :].broadcast_to([P, 2, S])
                crossed = rope_q_sb[:, k, 3 - 2 * j:4 - 2 * j, :].broadcast_to([P, 2, S])
                nc.vector.tensor_tensor(roped[:, j, k, :].rearrange("p (b s) -> p b s", b=2), q, straight, ALU.mult)
                last = nc.vector.tensor_tensor(cross[:, done % 2, 1 - j, :].rearrange("p (b s) -> p b s", b=2), q,
                                               crossed, ALU.mult)
                last.then_inc(ring_free, 1)

            def add_attention(u, n, c, w):
                dve.wait_ge(ring_full, u + 1)
                nc.vector.tensor_tensor(x_sb[:, c:c + w, :], bank(u)[:, 0:w * D].rearrange("p (c d) -> p c d", c=w),
                                        x_sb[:, c:c + w, :], ALU.add).then_inc(ring_free, 1)
                if n >= STEPS - 2:
                    dve.wait_ge(ring_free, freed[u])
                    variances(c, w, stats2_ready, moments2_ready, var2_ready)

            def context_low(q):
                n, head, b = item_of(2 * q)
                at = (slice(None), n % 2, head // 2, slice(b * S, (b + 1) * S))
                dve.wait_ge(context_hi_ready, q + 1)
                nc.vector.tensor_tensor(context_lo[at], context[:, 0:S], context_hi[at].bitcast(F32), ALU.subtract
                                        ).then_inc(context_lo_ready, 1)

            def maxima2(u, c, w):
                dve.wait_ge(ring_full, u + 1)
                nc.vector.tensor_reduce(neg_max2[:, c:c + w], bank(u)[:, 0:w * E].rearrange("p (c e) -> p c e", c=w),
                                        AX_X, ALU.max, negate=True).then_inc(max2_ready, w)

            def take_experts(c, w):
                end = c + w
                dve.wait_ge(ring_copied, freed_by[("logit", c, w)])
                for e in range(c, end):
                    last = nc.vector.max(top8[:, e, :], expo[:, e, :])
                last.then_inc(top_ready, w)
                nc.vector.reciprocal(inv2[:, c:end], sum2[:, c:end]).then_inc(inv2_ready, w)
                dve.wait_ge(top_ready, end)
                for e in range(c, end):
                    last = nc.vector.match_replace(out=rest[:, e, :], in_to_replace=top8[:, e, :],
                                                   in_values=expo[:, e, :], imm_value=0.0)
                last.then_inc(rest_ready, w)
                nc.vector.tensor_reduce(top_sum[:, c:end], top8[:, c:end, :], AX_X, ALU.add
                                        ).then_inc(top_sum_ready, w)
                dve.wait_ge(rest_ready, end)
                nc.vector.tensor_tensor(taken[:, c:end, :], expo[:, c:end, :], rest[:, c:end, :], ALU.subtract
                                        ).then_inc(taken_ready, w)

            def scales(c, w):
                end = c + w
                dve.wait_ge(inv2_ready, end)
                nc.vector.tensor_tensor(scale_e[:, c:end], inv2[:, c:end], tanh_gates[:, 1:2].broadcast_to([P, w]),
                                        ALU.mult)
                dve.wait_ge(top_sum_ready, end)
                nc.vector.scalar_tensor_tensor(out=scale_x[:, c:end], in0=inv2[:, c:end], scalar=tanh_gates[:, 1:2],
                                               in1=top_sum[:, c:end], op0=ALU.mult, op1=ALU.mult
                                               ).then_inc(scales_ready, w)
                if c < SHARED_FROM:
                    dve.wait_ge(scales_ready, end)
                    for e in range(c, end):
                        last = nc.vector.scalar_tensor_tensor(out=x_sb[:, e, :], in0=xn2[:, e, :],
                                                              scalar=scale_x[:, e:e + 1], in1=x_sb[:, e, :],
                                                              op0=ALU.mult, op1=ALU.add)
                    last.then_inc(partial, w)

            def finish(u, c, w):
                dve.wait_ge(ring_full, u + 1)
                if c < SHARED_FROM:
                    dve.wait_ge(partial, c + w)
                else:
                    dve.wait_ge(shared_partial, c + w - SHARED_FROM)
                for e in range(w):
                    last = nc.vector.scalar_tensor_tensor(out=x_sb[:, c + e, :], in0=bank(u)[:, e * D:(e + 1) * D],
                                                          scalar=scale_e[:, c + e:c + e + 1], in1=x_sb[:, c + e, :],
                                                          op0=ALU.mult, op1=ALU.add)
                last.then_inc(ring_free, 1)

            def pieces(slot):
                for u, piece in slot:
                    kind = piece[0]
                    if kind == "x":
                        _, t, dc = piece
                        cols = slice(t * SPAN, (t + 1) * SPAN)
                        last = low(xn_lo[:, dc, cols], bank(u), xn_hi[:, dc, cols], piece)
                        last.then_inc(ring_free, 1)
                    elif kind == "k":
                        cols = slice(piece[1] * 512, (piece[1] + 1) * 512)
                        low(keys_lo[:, cols], bank(u), keys_hi[:, cols], piece).then_inc(ring_free, 1)
                    elif kind == "a":
                        _, g, hh = piece
                        at = (slice(None), g % 2, slice(None), slice(None), slice(hh * HALF, (hh + 1) * HALF))
                        src = bank(u)[:, 0:2 * CQ].rearrange("p (c j r) -> p c j r", c=2, j=2)
                        low(a_lo[at], src, a_hi[at], piece).then_inc(ring_free, 1)
                    elif kind == "o":
                        g = piece[1]
                        dve.wait_ge(hi_ready, hi_count[piece])
                        product = bank(u).rearrange("p (a d) -> p a d", a=2)
                        nc.vector.scalar_tensor_tensor(out=o_lo[:, g % 2], in0=product,
                                                       scalar=tanh_gates[:, 0:1], in1=o_hi[:, g % 2].bitcast(F32),
                                                       op0=ALU.mult, op1=ALU.subtract).then_inc(ring_free, 1)
                    elif kind == "q":
                        _, n, k, j = piece
                        rope(n, k, j, u)
                    elif kind == "n":
                        layer_norm(piece[1])
                    elif kind == "out":
                        add_attention(u, *piece[1:])
                    elif kind == "norm":
                        normalise(xn2, *piece[1:], rstd2_ready, xn2_ready)
                    elif kind == "logit":
                        maxima2(u, *piece[1:])
                    elif kind == "take":
                        take_experts(*piece[1:])
                    elif kind == "part":
                        scales(*piece[1:])
                    elif kind == "mix":
                        finish(u, *piece[1:])
                    elif kind == "p":
                        for pair in range(2):
                            h0, h1 = 2 * pair, 2 * pair + 1
                            b = bank(u - 1 + pair)
                            low(q_stack[64:128, h0, :], b[0:64, :], q_stack[0:64, h0, :], piece, pair)
                            low(q_stack[0:64, h1, :], b[64:128, :], q_stack[64:128, h1, :], piece, pair
                                ).then_inc(ring_free, 1)

            def maxima(i):
                dve.wait_ge(scores_ready, i + 1)
                nc.vector.tensor_reduce(neg_max[:, i % 4, :], scores[:, i % 2], AX_X, ALU.max,
                                        negate=True).then_inc(max_ready, 1)

            def inverse(i):
                dve.wait_ge(exp_ready, i + 1)
                nc.vector.reciprocal(inv_sum[:, i % 4, :], row_sum[:, i % 4, :]).then_inc(inv_ready, 1)

            pieces(before)
            for i in range(LEAD):
                maxima(i)
            inverse(0)
            pieces(start)
            for n in range(STEPS):
                for s in range(ITEMS):
                    i = n * ITEMS + s
                    if i + 1 < items:
                        inverse(i + 1)
                    if i + LEAD < items and s != 6:
                        maxima(i + LEAD)
                    if i >= 3 and i % 2 == 1:
                        context_low(i // 2 - 1)
                    pieces(steps[n][s][0])
                    if i + LEAD < items and s == 6:
                        maxima(i + LEAD)
                    pieces(steps[n][s][1])
            context_low(items // 2 - 1)
            pieces(after)

        @block.tensor
        def _(pe):
            def free(u):
                if u >= RING and by_scalar[u - RING]:
                    pe.wait_ge(ring_copied, freed[u - RING])
                elif u >= RING:
                    pe.wait_ge(ring_free, freed[u - RING])

            def piece_done(u, last):
                last.then_inc(ring_full, 1)

            def turn_x(u, t, dc):
                for i in range(4):
                    c = 4 * t + i
                    pe.wait_ge(xn_ready, c // 2 * 2 + 2)
                    last = nc.tensor.transpose(bank(u)[:, i * P:(i + 1) * P], xn[:, c, dc * P:(dc + 1) * P], ident[:])
                piece_done(u, last)

            def turn_keys(u, i):
                pe.wait_ge(keys_ready, 1)
                for c in range(4):
                    last = nc.tensor.transpose(bank(u)[:, c * P:(c + 1) * P],
                                               keys[:, 4 * i + c].rearrange("p a d -> p (a d)"), ident[:])
                piece_done(u, last)

            def merge_queries(u, g, hh):
                pe.wait_ge(wq_in[g], 32)
                for dc in range(2):
                    last = nc.tensor.matmul(bank(u)[:, dc * CQ:(dc + 1) * CQ], wq_sb[:, hh, dc * P:(dc + 1) * P],
                                            w_kc_q_sb[:, hh, :], start=True, stop=True)
                piece_done(u, last)

            def merge_ranks(u, g, j):
                pe.wait_ge(wr_in[g], 32)
                for k in range(PC):
                    last = nc.tensor.matmul(bank(u)[:, k * P:(k + 1) * P], w_qr_sb[:, j, k, :], w_kr_sb[:, k, :],
                                            start=True, stop=True)
                piece_done(u, last)

            def merge_outputs(u, g, _):
                pe.wait_ge(wo_in[g], 32)
                for pair in range(2):
                    for e in range(2):
                        hh = 2 * pair + e
                        last = nc.tensor.matmul(bank(u)[64 * e:64 * e + 64, pair * D:(pair + 1) * D],
                                                w_kc_kv_sb[:, hh, :], wo_t_sb[:, hh, :], start=True, stop=True)
                piece_done(u, last)

            def project(u, n, k, j):
                g, t = n // 2, n % 2
                pe.wait_ge(ring_free, freed_by[("a", g, GH - 1)])
                pe.wait_ge(ring_free, freed_by[("x", t, 1)])
                cols = slice(t * SPAN, (t + 1) * SPAN)
                terms = [(a, xx, dc) for dc in range(2) for a, xx in ((a_hi, xn_hi), (a_hi, xn_lo), (a_lo, xn_hi))]
                for i, (a, xx, dc) in enumerate(terms):
                    last = nc.tensor.matmul(bank(u), a[:, g % 2, dc, j, k * P:(k + 1) * P], xx[:, dc, cols],
                                            start=(i == 0), stop=(i == len(terms) - 1))
                piece_done(u, last)

            def rank_chunk(u, n, k):
                g = n // 2
                pe.wait_ge(ring_copied, freed_by[("m", g, 1)])
                pe.wait_ge(rope_ready, n * PC + k + 1)
                for j in range(2):
                    nc.tensor.matmul(bank(u), m_sb[:, g % 2, j, k, :], roped[:, j, k, :], start=(j == 0), stop=False,
                                     skip_group_check=True)

            def start_rank_queries(u, n):
                rank_chunk(u, n, 0)

            def rank_queries(u, n):
                rank_chunk(u, n, 2)
                m = m_sb[:, (n // 2) % 2]
                for j in range(2):
                    first = nc.tensor.matmul(bank(u - 1)[64:128, :], m[0:64, j, 1, 0:64], roped[0:64, j, 1, :],
                                             start=False, stop=(j == 1), skip_group_check=True)
                    second = nc.tensor.matmul(bank(u)[0:64, :], m[64:128, j, 1, 64:128], roped[64:128, j, 1, :],
                                              start=False, stop=(j == 1), skip_group_check=True)
                piece_done(u - 1, first)
                piece_done(u, second)

            def attention_out(u, n, c, w):
                pe.wait_ge(context_lo_ready, last_item(n, batch=c // 2 % 2) // 2 + 1)
                pe.wait_ge(ring_free, freed_by[("o", n // 2, 0)])
                terms = [(cc, oo, pair) for pair in range(2)
                         for cc, oo in ((context_hi, o_hi), (context_hi, o_lo), (context_lo, o_hi))]
                for e in range(w):
                    cols = slice((c % 4 + e) * P, (c % 4 + e + 1) * P)
                    for i, (cc, oo, pair) in enumerate(terms):
                        last = nc.tensor.matmul(bank(u)[:, e * D:(e + 1) * D], cc[:, n % 2, pair, cols],
                                                oo[:, n // 2 % 2, pair, :], start=(i == 0),
                                                stop=(i == len(terms) - 1))
                piece_done(u, last)

            def turn_xn2(u, c, w):
                pe.wait_ge(xn2_ready, c + w)
                for e in range(w):
                    for dc in range(2):
                        at = (2 * e + dc) * P
                        last = nc.tensor.transpose(bank(u)[:, at:at + P], xn2[:, c + e, dc * P:(dc + 1) * P],
                                                   ident[:])
                piece_done(u, last)

            def logits(u, c, w):
                if c == 0:
                    pe.wait_ge(ffn_in, 48)
                pe.wait_ge(ring_copied, freed_by[("turn", c, w)])
                for e in range(w):
                    to = bank(u)[:, e * E:(e + 1) * E]
                    nc.tensor.matmul(to, ones[:], router_b_sb[:], start=True, stop=False)
                    for dc in range(2):
                        last = nc.tensor.matmul(to, xn2_t[:, (c + e) % 4, dc, :], router_t_sb[:, dc, :],
                                                start=False, stop=(dc == 1))
                piece_done(u, last)

            def turn_taken(u, c, w):
                pe.wait_ge(taken_ready, c + w)
                for e in range(w):
                    last = nc.tensor.transpose(bank(u)[0:E, e * P:(e + 1) * P], taken[:, c + e, :], ident[:])
                piece_done(u, last)

            def mix_experts(u, c, w):
                pe.wait_ge(ring_copied, freed_by[("pick", c, w)])
                for e in range(w):
                    last = nc.tensor.matmul(bank(u)[:, e * D:(e + 1) * D], taken_t[:, (c + e) % 4, :],
                                            expert_b_sb[:], start=True, stop=True)
                piece_done(u, last)

            def pieces(slot):
                for u, piece in slot:
                    if piece[0] in NO_BANK:
                        continue
                    free(u)
                    {"x": turn_x, "k": turn_keys, "a": merge_queries, "m": merge_ranks, "o": merge_outputs,
                     "q": project, "r": start_rank_queries, "p": rank_queries, "out": attention_out,
                     "turn": turn_xn2, "logit": logits, "pick": turn_taken, "mix": mix_experts
                     }[piece[0]](u, *piece[1:])

            def make_scores(i):
                n, head, b = item_of(i)
                pe.wait_ge(ring_free, freed_by[("p", n)] - 1 + head // 2)
                if i >= 2:
                    pe.wait_ge(exp_ready, i - 1)
                key = slice(((n % 2) * 2 + b) * L, ((n % 2) * 2 + b + 1) * L)
                for half in range(2):
                    q = q_stack[:, head, b * S + half * P:b * S + (half + 1) * P]
                    nc.tensor.matmul(scores[:, i % 2, half, :], q, keys_hi[:, key], start=True, stop=False)
                    last = nc.tensor.matmul(scores[:, i % 2, half, :], q, keys_lo[:, key], start=False, stop=True)
                last.then_inc(scores_ready, 1)

            def turn_probs(i):
                pe.wait_ge(probs_ready, i + 1)
                if i:
                    pe.wait_ge(probs_t_ready, i)
                for kc in range(2):
                    for half in range(2):
                        last = nc.tensor.transpose(probs_t[:, kc, half * P:(half + 1) * P],
                                                   probs[:, i % E_BUFS, half, kc * P:(kc + 1) * P], ident[:])
                last.then_inc(transposed, 1)

            def make_context(q):
                n, head, b = item_of(2 * q)
                pe.wait_ge(probs_t_ready, 2 * q + 2)
                if q:
                    pe.wait_ge(context_lo_ready, q)
                for kc in range(2):
                    for e in range(2):
                        last = nc.tensor.matmul(context[64 * e:64 * e + 64, 0:S],
                                                keys[:, ((n % 2) * 2 + b) * 2 + kc, 0, :],
                                                probs_t_sb[:, (2 * q + e) % T_BUFS, kc, :],
                                                start=(kc == 0), stop=(kc == 1))
                last.then_inc(context_ready, 1)

            pe.wait_ge(filled, 4)
            for _ in range(WARM_UP):
                nc.tensor.transpose(scores[:, 0, 0, 0:P], ident[:], ident[:])
            pieces(before)
            for i in range(LEAD):
                make_scores(i)
            pieces(start)
            for n in range(STEPS):
                for s in range(ITEMS):
                    i = n * ITEMS + s
                    if i >= 3 and i % 2 == 1:
                        make_context(i // 2 - 1)
                    if i + LEAD < items and s != 6:
                        make_scores(i + LEAD)
                    pieces(steps[n][s][0])
                    if i + LEAD < items and s == 6:
                        make_scores(i + LEAD)
                    turn_probs(i)
                    pieces(steps[n][s][1])
            make_context(items // 2 - 1)

            pieces(after)


def rope_rows(length, dim):
    inv = np.float32(1.0) / np.float32(10000.0) ** (np.arange(0, dim, 2, dtype=np.float32) / np.float32(dim))
    f = np.arange(length, dtype=np.float32)[:, None] * inv[None, :].astype(np.float32)
    return np.repeat(np.sin(f), 2, axis=-1).astype(np.float32), np.repeat(np.cos(f), 2, axis=-1).astype(np.float32)


def rope_tables():
    sin, cos = rope_rows(S, CQ)
    q = np.zeros((P, PC, 4, S), np.float32)
    for k in range(PC):
        c = (k * P + np.arange(P)) % HALF
        q[:, k, 0], q[:, k, 1] = cos[:, c].T, -sin[:, c].T
        q[:, k, 2], q[:, k, 3] = cos[:, c + HALF].T, sin[:, c + HALF].T
    sin, cos = rope_rows(L, DC)
    sin = np.concatenate([-sin[:, :DC // 2], sin[:, DC // 2:]], axis=1)
    k = np.stack([cos, sin], axis=1).reshape(2, P, 2, DC).transpose(1, 0, 2, 3)
    return q, np.ascontiguousarray(k)


def lay_out(inputs):
    w_qr, w_kr = np.asarray(inputs["L0_xattn_W_qr"]), np.asarray(inputs["L0_xattn_W_kr"])
    qr = np.zeros((GROUPS, 2, R, 2, PC, P), np.float32)
    kr = np.zeros((GROUPS, 2, R, PC, 2, DC), np.float32)
    for g in range(GROUPS):
        for k in range(PC):
            for p in range(P):
                hh, c = divmod(k * P + p, HALF)
                for j in range(2):
                    qr[g, hh - k, :, j, k, p] = w_qr[g * GH + hh, c + HALF * j, :]
            for slot in range(2):
                kr[g, slot, :, k, slot, :] = w_kr[g * GH + k + slot].T
    rope_q, rope_k = rope_tables()
    c = np.ascontiguousarray
    return {
        "x": c(np.asarray(inputs["x"]).reshape(TOKENS, D)),
        "ctx": c(np.asarray(inputs["ctx_512"]).reshape(B * L, DC)),
        "gate_attn": c(inputs["g_xattn"]),
        "gate_ffn": c(inputs["g_ffn"]),
        "wq": c(np.asarray(inputs["L0_xattn_Wq"]).reshape(H, K, D)),
        "w_kc_q": c(inputs["L0_xattn_w_kc_q"]),
        "w_kc_kv": c(inputs["L0_xattn_w_kc_kv"]),
        "w_qr": qr.reshape(GROUPS, P, 2, PC, P),
        "w_kr": kr.reshape(GROUPS, P, PC, P),
        "wo_t": c(np.asarray(inputs["L0_xattn_Wo"]).T.reshape(H, K, D)),
        "router_t": c(np.asarray(inputs["L0_ffn_router_weight"]).T),
        "router_b": c(inputs["L0_ffn_router_bias"]),
        "expert_b": c(inputs["L0_ffn_expert_bias"]),
        "rope_q": rope_q,
        "rope_k": rope_k,
    }


def kernel(**inputs):
    import concourse.bacc as bacc
    from concourse.bass_utils import run_bass_kernel_spmd

    arrays = lay_out(inputs)
    nc = bacc.Bacc("TRN2", target_bir_lowering=False, num_devices=1)
    args = [nc.dram_tensor(f"in_{n}", a.shape, mybir.dt.from_np(a.dtype), kind="ExternalInput").ap()
            for n, a in arrays.items()]
    out = nc.dram_tensor("out", (TOKENS, D), F32, kind="ExternalOutput").ap()
    flamingo_gated_layer(nc, *args, out)
    r = run_bass_kernel_spmd(nc, [{f"in_{n}": a for n, a in arrays.items()}], core_ids=[0])
    return r.results[0]["out"].reshape(B, S, D)
```
